# Optimizing a Trainium2 kernel written in Bass

```python
import numpy as np
import jax
import jax.numpy as jnp

def _softmax(x, axis=-1):
    return jax.nn.softmax(x, axis=axis)

def _gelu(x):
    return jax.nn.gelu(x, approximate=True)

def _silu(x):
    return jax.nn.silu(x)

def _sigmoid(x):
    return jax.nn.sigmoid(x)

def _layernorm(x, axis=-1, eps=1e-05):
    m = jnp.mean(x, axis=axis, keepdims=True)
    v = jnp.var(x, axis=axis, keepdims=True)
    return (x - m) / jnp.sqrt(v + eps)

def _scatter_add(tgt, idx, src, axis=0):
    return tgt.at[idx].add(src)

def _segment_sum(src, seg, n):
    return jax.ops.segment_sum(src, seg, n)
kernel_name = 'mk_gnn_ffn_d2_gnn_r8_821e35'

def setup_inputs(seed: int=0):
    np.random.seed(seed)
    _w = jnp.asarray

    def _rec_inputs():
        import jax
        import jax.numpy as jnp
        _gk = jax.random.key(seed)
        x = -0.0003713 + 1 * jax.random.normal(jax.random.fold_in(_gk, 1), (6250, 256), jnp.float32)
        _s = jax.random.randint(jax.random.fold_in(_gk, 2), (50000,), 0, 6250, jnp.int32)
        _d = jax.random.randint(jax.random.fold_in(_gk, 3), (50000,), 0, 6250, jnp.int32)
        _loop = jnp.arange(6250, dtype=jnp.int32)
        src = jnp.concatenate([_s, _d, _loop])
        dst = jnp.concatenate([_d, _s, _loop])
        _o = jnp.argsort(dst, stable=True)
        src = src[_o]
        dst = dst[_o]
        edge_attr_64 = -0.000128692 + 0.999872 * jax.random.normal(jax.random.fold_in(_gk, 12), (106250, 64), jnp.float32)
        return (x, src, dst, edge_attr_64)
    x, src, dst, edge_attr_64 = _rec_inputs()

    def _L0_gnn_setup():
        import jax, jax.numpy as jnp
        import numpy as np
        N_NODES = 6250
        N_EDGES = 100000
        IN_DIM = 256
        HEADS = 4
        HEAD_DIM = 64
        NEG_SLOPE = 0.2
        key = jax.random.key(seed)
        k1, k2, k3, k4, k5 = jax.random.split(key, 5)
        x = jax.random.normal(k1, (N_NODES, IN_DIM), dtype=jnp.float32)
        edge_index = jax.random.randint(k2, (2, N_EDGES), 0, N_NODES, dtype=jnp.int64)
        W = jax.random.normal(k3, (IN_DIM, HEADS * HEAD_DIM), dtype=jnp.float32) * (1.0 / np.sqrt(IN_DIM))
        att_src = jax.random.normal(k4, (HEADS, HEAD_DIM), dtype=jnp.float32) * (1.0 / np.sqrt(HEAD_DIM))
        att_dst = jax.random.normal(k5, (HEADS, HEAD_DIM), dtype=jnp.float32) * (1.0 / np.sqrt(HEAD_DIM))
        bias = jnp.zeros((HEADS * HEAD_DIM,), dtype=jnp.float32)
        return {'x': x, 'edge_index': edge_index, 'W': W, 'att_src': att_src, 'att_dst': att_dst, 'bias': bias}
    _L0_gnn_all = _L0_gnn_setup()
    _L0_gnn_in = {k: v for k, v in _L0_gnn_all.items() if k in ('W', 'att_src', 'att_dst', 'bias')}
    del _L0_gnn_all

    def _L0_ffn_setup():
        import jax, jax.numpy as jnp
        import numpy as np
        E, D, H, TOP_K = (6, 256, 256, 2)
        ROUTER_H = D // 2
        key = jax.random.key(seed)
        ks = jax.random.split(key, 12)
        s = 1.0 / np.sqrt(D)
        sh = 1.0 / np.sqrt(H)
        sr = 1.0 / np.sqrt(ROUTER_H)
        return {'features': jax.random.normal(ks[0], (8, 512, D), dtype=jnp.float32), 'router_w1': jax.random.uniform(ks[1], (D, ROUTER_H), jnp.float32, -s, s), 'router_b1': jnp.zeros((ROUTER_H,), jnp.float32), 'router_w2': jax.random.uniform(ks[2], (ROUTER_H, E), jnp.float32, -sr, sr), 'router_b2': jnp.zeros((E,), jnp.float32), 'expert_w1': jax.random.uniform(ks[3], (E, D, H), jnp.float32, -s, s), 'expert_b1': jnp.zeros((E, H), jnp.float32), 'expert_w2': jax.random.uniform(ks[4], (E, H, H), jnp.float32, -sh, sh), 'expert_b2': jnp.zeros((E, H), jnp.float32), 'expert_w3': jax.random.uniform(ks[5], (E, H, D), jnp.float32, -sh, sh), 'expert_b3': jnp.zeros((E, D), jnp.float32)}
    _L0_ffn_all = _L0_ffn_setup()
    _L0_ffn_in = {k: v for k, v in _L0_ffn_all.items() if k in ('router_w1', 'router_b1', 'router_w2', 'router_b2', 'expert_w1', 'expert_b1', 'expert_w2', 'expert_b2', 'expert_w3', 'expert_b3')}
    del _L0_ffn_all

    def _L1_gnn_setup():
        import jax, jax.numpy as jnp
        import numpy as np
        N_NODES = 2500
        N_EDGES = 80000
        IN_CH = 256
        OUT_CH = 256
        EDGE_DIM = 64
        key = jax.random.key(seed)
        ks = jax.random.split(key, 8)
        x = jax.random.normal(ks[0], (N_NODES, IN_CH), dtype=jnp.float32)
        edge_attr = jax.random.normal(ks[1], (N_EDGES, EDGE_DIM), dtype=jnp.float32)
        W1 = jax.random.normal(ks[2], (OUT_CH, IN_CH + EDGE_DIM), dtype=jnp.float32) * (1.0 / np.sqrt(IN_CH + EDGE_DIM))
        W2 = jax.random.normal(ks[3], (OUT_CH, IN_CH), dtype=jnp.float32) * (1.0 / np.sqrt(IN_CH))
        att_l = jax.random.normal(ks[4], (1, OUT_CH), dtype=jnp.float32) * (1.0 / np.sqrt(OUT_CH))
        att_r = jax.random.normal(ks[5], (1, IN_CH), dtype=jnp.float32) * (1.0 / np.sqrt(IN_CH))
        bias = jnp.zeros((OUT_CH,), dtype=jnp.float32)
        src = jax.random.randint(ks[6], (N_EDGES,), 0, N_NODES, dtype=jnp.int32)
        dst = jax.random.randint(ks[7], (N_EDGES,), 0, N_NODES, dtype=jnp.int32)
        return {'x': x, 'edge_attr': edge_attr, 'W1': W1, 'W2': W2, 'att_l': att_l, 'att_r': att_r, 'bias': bias, 'src': src, 'dst': dst}
    _L1_gnn_all = _L1_gnn_setup()
    _L1_gnn_in = {k: v for k, v in _L1_gnn_all.items() if k in ('W1', 'W2', 'att_l', 'att_r', 'bias')}
    del _L1_gnn_all

    def _L1_ffn_setup():
        import jax, jax.numpy as jnp
        import numpy as np
        BN_EPS = 0.001

        def _bn(h, g, b, m, v):
            return g * (h - m) * jax.lax.rsqrt(v + BN_EPS) + b
        key = jax.random.key(seed)
        ks = jax.random.split(key, 8)
        B, F, Df = (256, 64, 256)
        E, H, D = (8, 256, 256)
        s1 = 1.0 / np.sqrt(Df)
        s2 = 1.0 / np.sqrt(H)
        return {'x': jax.random.normal(ks[0], (B, F, Df), jnp.float32), 'Wr': jax.random.normal(ks[1], (Df, E), jnp.float32) * s1, 'br': jnp.zeros((E,), jnp.float32), 'W1': jax.random.normal(ks[2], (E, Df, H), jnp.float32) * s1, 'b1': jnp.zeros((E, H), jnp.float32), 'g1': jnp.ones((E, H), jnp.float32), 'be1': jnp.zeros((E, H), jnp.float32), 'm1': jnp.zeros((E, H), jnp.float32), 'v1': jnp.ones((E, H), jnp.float32), 'W2': jax.random.normal(ks[3], (E, H, H), jnp.float32) * s2, 'b2': jnp.zeros((E, H), jnp.float32), 'g2': jnp.ones((E, H), jnp.float32), 'be2': jnp.zeros((E, H), jnp.float32), 'm2': jnp.zeros((E, H), jnp.float32), 'v2': jnp.ones((E, H), jnp.float32), 'Wo': jax.random.normal(ks[4], (E, H, D), jnp.float32) * s2, 'bo': jnp.zeros((E, D), jnp.float32)}
    _L1_ffn_all = _L1_ffn_setup()
    _L1_ffn_in = {k: v for k, v in _L1_ffn_all.items() if k in ('Wr', 'br', 'W1', 'b1', 'g1', 'be1', 'm1', 'v1', 'W2', 'b2', 'g2', 'be2', 'm2', 'v2', 'Wo', 'bo')}
    del _L1_ffn_all
    return {'x': x, 'src': src, 'dst': dst, 'edge_attr_64': edge_attr_64, 'L0_gnn_W': _L0_gnn_in['W'], 'L0_gnn_att_src': _L0_gnn_in['att_src'], 'L0_gnn_att_dst': _L0_gnn_in['att_dst'], 'L0_gnn_bias': _L0_gnn_in['bias'], 'L0_ffn_router_w1': _L0_ffn_in['router_w1'], 'L0_ffn_router_b1': _L0_ffn_in['router_b1'], 'L0_ffn_router_w2': _L0_ffn_in['router_w2'], 'L0_ffn_router_b2': _L0_ffn_in['router_b2'], 'L0_ffn_expert_w1': _L0_ffn_in['expert_w1'], 'L0_ffn_expert_b1': _L0_ffn_in['expert_b1'], 'L0_ffn_expert_w2': _L0_ffn_in['expert_w2'], 'L0_ffn_expert_b2': _L0_ffn_in['expert_b2'], 'L0_ffn_expert_w3': _L0_ffn_in['expert_w3'], 'L0_ffn_expert_b3': _L0_ffn_in['expert_b3'], 'L1_gnn_W1': _L1_gnn_in['W1'], 'L1_gnn_W2': _L1_gnn_in['W2'], 'L1_gnn_att_l': _L1_gnn_in['att_l'], 'L1_gnn_att_r': _L1_gnn_in['att_r'], 'L1_gnn_bias': _L1_gnn_in['bias'], 'L1_ffn_Wr': _L1_ffn_in['Wr'], 'L1_ffn_br': _L1_ffn_in['br'], 'L1_ffn_W1': _L1_ffn_in['W1'], 'L1_ffn_b1': _L1_ffn_in['b1'], 'L1_ffn_g1': _L1_ffn_in['g1'], 'L1_ffn_be1': _L1_ffn_in['be1'], 'L1_ffn_m1': _L1_ffn_in['m1'], 'L1_ffn_v1': _L1_ffn_in['v1'], 'L1_ffn_W2': _L1_ffn_in['W2'], 'L1_ffn_b2': _L1_ffn_in['b2'], 'L1_ffn_g2': _L1_ffn_in['g2'], 'L1_ffn_be2': _L1_ffn_in['be2'], 'L1_ffn_m2': _L1_ffn_in['m2'], 'L1_ffn_v2': _L1_ffn_in['v2'], 'L1_ffn_Wo': _L1_ffn_in['Wo'], 'L1_ffn_bo': _L1_ffn_in['bo']}

def reference(x, src, dst, edge_attr_64, L0_gnn_W, L0_gnn_att_src, L0_gnn_att_dst, L0_gnn_bias, L0_ffn_router_w1, L0_ffn_router_b1, L0_ffn_router_w2, L0_ffn_router_b2, L0_ffn_expert_w1, L0_ffn_expert_b1, L0_ffn_expert_w2, L0_ffn_expert_b2, L0_ffn_expert_w3, L0_ffn_expert_b3, L1_gnn_W1, L1_gnn_W2, L1_gnn_att_l, L1_gnn_att_r, L1_gnn_bias, L1_ffn_Wr, L1_ffn_br, L1_ffn_W1, L1_ffn_b1, L1_ffn_g1, L1_ffn_be1, L1_ffn_m1, L1_ffn_v1, L1_ffn_W2, L1_ffn_b2, L1_ffn_g2, L1_ffn_be2, L1_ffn_m2, L1_ffn_v2, L1_ffn_Wo, L1_ffn_bo):
    import jax
    import jax.numpy as jnp

    def _L0_gnn_ref(x, edge_index, W, att_src, att_dst, bias):
        import jax, jax.numpy as jnp
        import numpy as np
        N_NODES = 6250
        N_EDGES = 100000
        IN_DIM = 256
        HEADS = 4
        HEAD_DIM = 64
        NEG_SLOPE = 0.2
        N = x.shape[0]
        loops = jnp.arange(N, dtype=edge_index.dtype)
        src = jnp.concatenate([edge_index[0], loops])
        dst = jnp.concatenate([edge_index[1], loops])
        h = (x @ W).reshape(N, HEADS, HEAD_DIM)
        a_src = jnp.einsum('nhd,hd->nh', h, att_src)
        a_dst = jnp.einsum('nhd,hd->nh', h, att_dst)
        e = a_src[src] + a_dst[dst]
        e = jax.nn.leaky_relu(e, NEG_SLOPE)
        m = jax.ops.segment_max(e, dst, num_segments=N)
        e = jnp.exp(e - m[dst])
        denom = jax.ops.segment_sum(e, dst, num_segments=N)
        alpha = e / denom[dst]
        msg = alpha[:, :, None] * h[src]
        out = jax.ops.segment_sum(msg, dst, num_segments=N)
        return out.reshape(N, HEADS * HEAD_DIM) + bias

    def _L0_ffn_ref(features, router_w1, router_b1, router_w2, router_b2, expert_w1, expert_b1, expert_w2, expert_b2, expert_w3, expert_b3):
        import jax, jax.numpy as jnp
        import numpy as np
        E, D, H, TOP_K = (6, 256, 256, 2)
        ROUTER_H = D // 2
        rh = jax.nn.relu(features @ router_w1 + router_b1)
        expert_logits = jax.nn.softmax(rh @ router_w2 + router_b2, axis=-1)
        top_w, top_i = jax.lax.top_k(expert_logits, TOP_K)
        routing_weights = jax.nn.softmax(top_w, axis=-1)
        h1 = jax.nn.relu(jnp.einsum('bsd,edh->bseh', features, expert_w1) + expert_b1)
        h2 = jax.nn.relu(jnp.einsum('bseh,ehf->bsef', h1, expert_w2) + expert_b2)
        expert_out = jnp.einsum('bsef,efo->bseo', h2, expert_w3) + expert_b3
        sel = jnp.take_along_axis(expert_out, top_i[:, :, :, None], axis=2)
        combined = jnp.sum(sel * routing_weights[..., None], axis=2)
        return combined

    def _L1_gnn_ref(x, edge_attr, W1, W2, att_l, att_r, bias, src, dst):
        import jax, jax.numpy as jnp
        import numpy as np
        N_NODES = 2500
        N_EDGES = 80000
        IN_CH = 256
        OUT_CH = 256
        EDGE_DIM = 64
        n = x.shape[0]
        x_t = x @ W2.T
        ar = (x * att_r).sum(-1)
        er = ar[dst]
        x_e = x[src]
        f = jnp.concatenate([x_e, edge_attr], axis=-1) @ W1.T
        el = (f * att_l).sum(-1)
        score = jax.nn.leaky_relu(er + el)
        seg_max = jax.ops.segment_max(score, dst, num_segments=n)
        e = jnp.exp(score - seg_max[dst])
        seg_sum = jax.ops.segment_sum(e, dst, num_segments=n)
        alpha = e / seg_sum[dst]
        msg = x_t[src] * alpha[:, None]
        h = jax.ops.segment_sum(msg, dst, num_segments=n)
        return h + bias

    def _L1_ffn_ref(x, Wr, br, W1, b1, g1, be1, m1, v1, W2, b2, g2, be2, m2, v2, Wo, bo):
        import jax, jax.numpy as jnp
        import numpy as np
        BN_EPS = 0.001

        def _bn(h, g, b, m, v):
            return g * (h - m) * jax.lax.rsqrt(v + BN_EPS) + b
        feat = jnp.mean(x, axis=0)
        w = jax.nn.softmax(feat @ Wr + br, axis=-1)
        h = jnp.einsum('bfd,edh->bfeh', x, W1) + b1
        h = jax.nn.relu(_bn(h, g1, be1, m1, v1))
        h = jnp.einsum('bfeh,ehk->bfek', h, W2) + b2
        h = jax.nn.relu(_bn(h, g2, be2, m2, v2))
        y = jnp.einsum('bfeh,ehd->bfed', h, Wo) + bo
        return jnp.einsum('bfed,fe->bfd', y, w)
    edge_index = jnp.stack([src, dst])
    x = x + _L0_gnn_ref(_layernorm(x, axis=-1), edge_index, L0_gnn_W, L0_gnn_att_src, L0_gnn_att_dst, L0_gnn_bias)
    x = x + _L0_ffn_ref(_layernorm(x, axis=-1)[None], L0_ffn_router_w1, L0_ffn_router_b1, L0_ffn_router_w2, L0_ffn_router_b2, L0_ffn_expert_w1, L0_ffn_expert_b1, L0_ffn_expert_w2, L0_ffn_expert_b2, L0_ffn_expert_w3, L0_ffn_expert_b3)[0]
    x = x + _L1_gnn_ref(_layernorm(x, axis=-1), edge_attr_64, L1_gnn_W1, L1_gnn_W2, L1_gnn_att_l, L1_gnn_att_r, L1_gnn_bias, src, dst)
    x = x + _L1_ffn_ref(_layernorm(x, axis=-1)[None], L1_ffn_Wr, L1_ffn_br, L1_ffn_W1, L1_ffn_b1, L1_ffn_g1, L1_ffn_be1, L1_ffn_m1, L1_ffn_v1, L1_ffn_W2, L1_ffn_b2, L1_ffn_g2, L1_ffn_be2, L1_ffn_m2, L1_ffn_v2, L1_ffn_Wo, L1_ffn_bo)[0]
    return x

_drawn_inputs = setup_inputs


def setup_inputs(seed=0):
    import zlib

    import numpy as np

    out = dict(_drawn_inputs(seed))
    spreads = {'L0_gnn_bias': (0.0, 0.1),
     'L0_ffn_router_b1': (0.0, 0.1),
     'L0_ffn_router_b2': (0.0, 0.1),
     'L0_ffn_expert_b1': (0.0, 0.667),
     'L0_ffn_expert_b2': (0.0, 0.278),
     'L0_ffn_expert_b3': (0.0, 0.1),
     'L1_gnn_bias': (0.0, 0.1),
     'L1_ffn_br': (0.0, 0.573),
     'L1_ffn_b1': (0.0, 0.342),
     'L1_ffn_g1': (1.0, 0.2),
     'L1_ffn_be1': (0.0, 0.371),
     'L1_ffn_m1': (0.0, 0.35),
     'L1_ffn_v1': (1.0, 0.6),
     'L1_ffn_b2': (0.0, 0.1),
     'L1_ffn_g2': (1.0, 0.2),
     'L1_ffn_be2': (0.0, 0.277),
     'L1_ffn_m2': (0.0, 0.1),
     'L1_ffn_v2': (1.0, 0.6),
     'L1_ffn_bo': (0.0, 0.1)}
    factors = {}
    for name, (base, spread) in spreads.items():
        noise = np.random.default_rng([zlib.crc32(name.encode()), seed]).standard_normal(out[name].shape)
        drawn = base * np.exp(spread * noise) if base else spread * noise
        out[name] = jnp.asarray(drawn.astype(out[name].dtype))
    for name, factor in factors.items():
        out[name] = (out[name] * factor).astype(out[name].dtype)
    return out
```

```python
from contextlib import ExitStack

import numpy as np
import concourse.bass as bass
from concourse import mybir

F32 = mybir.dt.float32
I32 = mybir.dt.int32
ALU = mybir.AluOpType
ACT = mybir.ActivationFunctionType
AX = mybir.AxisListType

P = 128
N = 6250
D = 256
TN = 125
NT = N // TN
E = 106250
EP = 125
EC = E // EP
C = 4
UE = P * C
UNITS = (E + (UE - 1) * NT) // UE
SU = (UNITS + 1) // 2
Q = 2 * C
LOG_UE = 9
EPAD = E + UE
AE = 64
RING = 4
LAG = 3
BODIES = (SU + LAG) // RING
GT = 2
GN = GT * TN
NG = NT // GT
BIG = 1.0e30
LN_EPS = 1e-5
BN_EPS = 1e-3
assert UE == 1 << LOG_UE and (SU + LAG) % RING == 0 and (NG + 1) % 2 == 0 and EP * EC == E

HEADS = (4, 1)
SLOPES = (0.2, 0.01)
EXPERTS = (6, 8)


def build(nc, a, out):
    ctx = ExitStack()
    with ctx:
        def sb(name, shape, dt=F32, scope=ctx):
            return scope.enter_context(nc.sbuf_tensor(name, shape, dt))

        sems = {}
        stage = [0]

        def S(name):
            if name not in sems:
                sems[name] = nc.alloc_semaphore(name=f"{name}_{stage[0]}")
            return sems[name]

        def end_stage():
            nc.clear_and_free_semaphores(list(sems.values()))
            sems.clear()
            stage[0] += 1
            nc.all_engine_barrier()

        def after(eng, name, count):
            if not isinstance(count, int) or count > 0:
                eng.wait_ge(S(name), count)

        def held(eng, name):
            eng.sem_inc(S(name), 1)

        def copy(out_, in_):
            return nc.vector.tensor_scalar(out_, in_, 1.0, None, ALU.mult)

        bank = [ctx.enter_context(nc.psum_tensor(f"bank{k}", [P, 512], F32)) for k in range(8)]

        pack_d = nc.dram_tensor("edge_pack", [EPAD, 2], I32).ap()
        dst_d = nc.dram_tensor("edge_dst", [EPAD], F32).ap()
        q_d = nc.dram_tensor("edge_q", [EPAD], F32).ap()
        unit_d = nc.dram_tensor("unit_table", [3 * P, 2], I32).ap()
        rows_d = [nc.dram_tensor(f"rows{l}", [N, HEADS[l] * (D // HEADS[l] + 1)], F32).ap() for l in (0, 1)]

        X = sb("X", [TN, NT, D])
        ident = sb("ident", [P, P])
        iota_n = sb("iota_n", [P, TN])
        nid = sb("nid", [P, NT])
        base = sb("base", [P, NT])
        ones = sb("ones", [P, P])
        unit_i = sb("unit_i", [1, 6 * P], I32)
        eps_ln = sb("eps_ln", [P, 1])
        eps_bn = sb("eps_bn", [P, 1])
        stats = sb("stats", [TN, 2, 6])
        aggr = sb("aggr", [TN, 2, 2])
        mv = sb("mv", [TN, NT, 2])
        std = sb("std", [TN, NT])
        rstd = sb("rstd", [TN, NT])
        ad = [sb(f"ad{l}", [TN, NT * HEADS[l]]) for l in (0, 1)]
        mrun = [sb(f"mrun{l}", [TN, NT * HEADS[l]]) for l in (0, 1)]
        ue_bc = sb("ue_bc", [EP, AE])

        with ExitStack() as sc:
            src_t = sb("src_t", [EP, EC], I32, sc)
            dst_t = sb("dst_t", [EP, EC], I32, sc)
            dstf = sb("dstf", [EP, EC], F32, sc)
            pack_t = sb("pack_t", [EP, EC, 2], I32, sc)
            pad_pack = sb("pad_pack", [P, C, 2], I32, sc)
            pad_f = sb("pad_f", [P, C], F32, sc)
            pad_q = sb("pad_q", [P, C], F32, sc)
            below = sb("below", [EP, EC], F32, sc)
            cnt = sb("cnt", [EP, NT + 1], F32, sc)
            int_n = sb("int_n", [P, TN], I32, sc)
            int_nid = sb("int_nid", [P, NT], I32, sc)
            int_base = sb("int_base", [P, NT], I32, sc)
            int_u = sb("int_u", [P, 3], I32, sc)
            uf = sb("uf", [P, 3], F32, sc)
            tile_f = sb("tile_f", [P, NT], F32, sc)
            int_tile = sb("int_tile", [P, NT], I32, sc)
            bound = sb("bound", [P, NT], F32, sc)
            zeros = sb("zeros", [P, NT], F32, sc)
            ptr = sb("ptr", [P, NT + 1], F32, sc)
            wide = sb("wide", [P, NT], F32, sc)
            wide_i = sb("wide_i", [P, NT], I32, sc)
            nunit_i = sb("nunit_i", [P, NT], I32, sc)
            nunit = sb("nunit", [P, NT], F32, sc)
            ends = sb("ends", [P, NT], F32, sc)
            starts = sb("starts", [P, NT], F32, sc)
            off = sb("off", [P, NT], F32, sc)
            ge = sb("ge", [P, 3, NT], F32, sc)
            jf = sb("jf", [P, 3], F32, sc)
            hot = sb("hot", [P, 3, NT], F32, sc)
            sf = sb("sf", [P, 3], F32, sc)
            sf2 = sb("sf2", [P, 3], F32, sc)
            unit_t = sb("unit_t", [P, 3, 2], I32, sc)
            w1a = sb("w1a", [P, 2, AE], F32, sc)
            attl = sb("attl", [P, 2, 1], F32, sc)
            attl_b = sb("attl_b", [P, 2, EP], F32, sc)
            EB = 34
            NE = EC // EB
            assert NE * EB == EC and NE % 2 == 1
            ea_t = sb("ea_t", [EP, 2, EB, AE], F32, sc)
            qp = sb("qp", [EP, EB, AE], F32, sc)
            q_t = sb("q_t", [EP, EC], F32, sc)
            ea_v = a["edge_attr_64"].rearrange("(p c) f -> p c f", p=EP)

            with nc.Block() as block:
                @block.sync
                def _(sp):
                    sp.dma_start(src_t[:, :], a["src"].rearrange("(p c) -> p c", p=EP)).then_inc(S("src_in"), 16)
                    sp.dma_start(dst_t[:, :], a["dst"].rearrange("(p c) -> p c", p=EP)).then_inc(S("dst_in"), 16)
                    sp.dma_start(X[:, :, :], a["x"].rearrange("(t p) d -> p t d", p=TN)).then_inc(S("x_in"), 16)
                    sp.wait_ge(S("pads_set"), 1)
                    sp.dma_start(pack_d[E:EPAD, :].rearrange("(p c) k -> p c k", p=P), pad_pack[:, :, :]).then_inc(S("pad_out"), 16)
                    sp.dma_start(dst_d[E:EPAD].rearrange("(p c) -> p c", p=P), pad_f[:, :]).then_inc(S("pad_out"), 16)
                    sp.dma_start(q_d[E:EPAD].rearrange("(p c) -> p c", p=P), pad_q[:, :]).then_inc(S("pad_out"), 16)
                    sp.wait_ge(S("pack_made"), 1)
                    sp.dma_start(pack_d[0:E, :].rearrange("(p c) k -> p c k", p=EP), pack_t[:, :, :]).then_inc(S("pack_out"), 16)
                    sp.dma_start(dst_d[0:E].rearrange("(p c) -> p c", p=EP), dstf[:, :]).then_inc(S("pack_out"), 16)
                    sp.wait_ge(S("units_made"), 1)
                    sp.dma_start(unit_d.rearrange("(p k) t -> p k t", p=P), unit_t[:, :, :]).then_inc(S("unit_out"), 16)
                    sp.wait_ge(S("unit_out"), 16)
                    sp.dma_start(unit_i[:, :], unit_d.rearrange("(o u) t -> o (u t)", o=1)).then_inc(S("unit_in"), 16)
                    sp.wait_ge(S("q_made"), 1)
                    sp.dma_start(q_d[0:E].rearrange("(p c) -> p c", p=EP), q_t[:, :]).then_inc(S("q_out"), 16)
                    sp.wait_ge(S("pad_out"), 48)
                    sp.wait_ge(S("pack_out"), 32)
                    sp.wait_ge(S("unit_in"), 16)
                    sp.wait_ge(S("q_out"), 16)
                    sp.wait_ge(S("x_in"), 16)

                @block.gpsimd
                def _(pool):
                    nc.gpsimd.memset(ident[:, :], 0.0).then_inc(S("ident_zero"), 1)
                    pool.wait_ge(S("ident_zero"), 1)
                    nc.gpsimd.affine_select(out=ident[:, :], in_=ident[:, :], compare_op=ALU.not_equal, fill=1.0,
                                            base=0, pattern=[[-1, P]], channel_multiplier=1).then_inc(S("ident_set"), 1)
                    nc.gpsimd.iota(int_n[:, :], pattern=[[1, TN]], base=0, channel_multiplier=0)
                    nc.gpsimd.iota(int_nid[:, :], pattern=[[TN, NT]], base=0, channel_multiplier=1)
                    nc.gpsimd.iota(int_base[:, :], pattern=[[TN, NT]], base=0, channel_multiplier=0)
                    nc.gpsimd.iota(int_tile[:, :], pattern=[[1, NT]], base=0, channel_multiplier=0)
                    nc.gpsimd.iota(int_u[:, :], pattern=[[1, 3]], base=0, channel_multiplier=3).then_inc(S("iotas"), 1)
                    nc.gpsimd.memset(ones[:, :], 1.0)
                    nc.gpsimd.memset(zeros[:, :], 0.0)
                    nc.gpsimd.memset(eps_ln[:, :], LN_EPS)
                    nc.gpsimd.memset(eps_bn[:, :], BN_EPS)
                    nc.gpsimd.memset(cnt[:, :], 0.0).then_inc(S("fills"), 1)
                    nc.gpsimd.memset(pad_f[:, :], -1.0)
                    nc.gpsimd.memset(pad_q[:, :], 0.0)
                    nc.gpsimd.memset(pad_pack[:, :, 0:1], 0)
                    nc.gpsimd.memset(pad_pack[:, :, 1:2].bitcast(F32), -1.0).then_inc(S("pads_set"), 1)

                @block.scalar
                def _(act):
                    act.dma_start(w1a[:, :, :], a["L1_gnn_W1"][:, D:D + AE].rearrange("(o p) f -> p o f", p=P)).then_inc(S("ue_in"), 16)
                    act.dma_start(attl[:, :, :], a["L1_gnn_att_l"].rearrange("z (o p) -> p o z", p=P), allow_slow_non_contiguous=True).then_inc(S("ue_in"), 16)
                    act.wait_ge(S("ue_mm"), 1)
                    nc.scalar.copy(ue_bc[:, :], bank[1][0:EP, 0:AE]).then_inc(S("ue_set"), 1)

                    def load_ea(k, slot):
                        act.dma_start(ea_t[:, slot, :, :], ea_v[:, bass.ds(k * EB, EB), :]).then_inc(S(f"ea_in{slot}"), 16)

                    load_ea(0, 0)
                    with act.Fori(0, NE // 2) as h:
                        load_ea(h * 2 + 1, 1)
                        act.wait_ge(S("ea_used"), h * 2 + 1)
                        load_ea(h * 2 + 2, 0)
                        act.wait_ge(S("ea_used"), h * 2 + 2)

                @block.tensor
                def _(pe):
                    pe.wait_ge(S("fills"), 1)
                    pe.wait_ge(S("counts"), 1)
                    nc.tensor.matmul(bank[0][:, 0:NT + 1], ones[0:EP, :], cnt[:, :], start=True, stop=True).then_inc(S("ptr_mm"), 1)
                    pe.wait_ge(S("attl_b"), 1)
                    for o in range(2):
                        mm = nc.tensor.matmul(bank[1][0:EP, 0:AE], attl_b[:, o, :], w1a[:, o, :], start=(o == 0), stop=(o == 1))
                    mm.then_inc(S("ue_mm"), 1)

                @block.vector
                def _(v):
                    v.wait_ge(S("iotas"), 1)
                    nc.vector.tensor_copy(iota_n[:, :], int_n[:, :])
                    nc.vector.tensor_copy(nid[:, :], int_nid[:, :])
                    nc.vector.tensor_copy(base[:, :], int_base[:, :]).then_inc(S("consts"), 1)
                    nc.vector.tensor_copy(uf[:, :], int_u[:, :])
                    nc.vector.tensor_copy(tile_f[:, :], int_tile[:, :])
                    v.wait_ge(S("consts"), 1)
                    nc.vector.tensor_scalar(bound[:, :], base[:, :], float(TN), None, ALU.add).then_inc(S("bound"), 1)
                    v.wait_ge(S("fills"), 1)
                    v.wait_ge(S("ue_in"), 32)
                    nc.vector.tensor_copy(attl_b[:, :, :], attl[:, :, :].broadcast_to([P, 2, EP])).then_inc(S("attl_b"), 1)
                    v.wait_ge(S("dst_in"), 16)
                    v.wait_ge(S("src_in"), 16)
                    nc.vector.tensor_copy(dstf[:, :], dst_t[:, :]).then_inc(S("dstf"), 1)
                    nc.vector.tensor_copy(pack_t[:, :, 0], src_t[:, :])
                    v.wait_ge(S("dstf"), 1)
                    nc.vector.tensor_copy(pack_t[:, :, 1].bitcast(F32), dstf[:, :]).then_inc(S("pack_made"), 1)
                    v.wait_ge(S("bound"), 1)
                    with v.Fori(0, NT) as t:
                        v.wait_ge(S("bound"), t + 1)
                        nc.vector.tensor_scalar(below[:, :], dstf[:, :], bound[0:EP, bass.ds(t, 1)], 0.0, ALU.is_lt, ALU.add,
                                                accum_out=cnt[:, bass.ds(t + 1, 1)]).then_inc(S("bound"), 1)
                    v.wait_ge(S("bound"), NT + 1)
                    v.sem_inc(S("counts"), 1)
                    v.wait_ge(S("ptr_mm"), 1)
                    k = [0]

                    def step(ins):
                        k[0] += 1
                        ins.then_inc(S("unit_step"), 1)
                        v.wait_ge(S("unit_step"), k[0])

                    step(nc.vector.tensor_copy(ptr[:, :], bank[0][:, 0:NT + 1]))
                    step(nc.vector.tensor_tensor(wide[:, :], ptr[:, 1:NT + 1], ptr[:, 0:NT], ALU.subtract))
                    step(nc.vector.tensor_scalar(wide_i[:, :], wide[:, :], float(UE - 1), None, ALU.add))
                    step(nc.vector.tensor_scalar(nunit_i[:, :], wide_i[:, :], LOG_UE, None, ALU.arith_shift_right))
                    step(nc.vector.tensor_copy(nunit[:, :], nunit_i[:, :]))
                    step(nc.vector.tensor_tensor_scan(ends[:, :], nunit[:, :], zeros[:, :], 0.0, ALU.add, ALU.add))
                    step(nc.vector.tensor_tensor(starts[:, :], ends[:, :], nunit[:, :], ALU.subtract))
                    step(nc.vector.scalar_tensor_tensor(off[:, :], starts[:, :], -float(UE), ptr[:, 0:NT], ALU.mult, ALU.add))
                    step(nc.vector.tensor_tensor(ge[:, :, :], uf[:, :].unsqueeze(2).broadcast_to([P, 3, NT]),
                                                 ends[:, :].unsqueeze(1).broadcast_to([P, 3, NT]), ALU.is_ge))
                    step(nc.vector.tensor_reduce(jf[:, :], ge[:, :, :], AX.X, ALU.add))
                    step(nc.vector.tensor_scalar(jf[:, :], jf[:, :], float(NT - 1), None, ALU.min))
                    step(nc.vector.tensor_tensor(hot[:, :, :], jf[:, :].unsqueeze(2).broadcast_to([P, 3, NT]),
                                                 tile_f[:, :].unsqueeze(1).broadcast_to([P, 3, NT]), ALU.is_equal))
                    step(nc.vector.tensor_tensor(hot[:, :, :], hot[:, :, :], off[:, :].unsqueeze(1).broadcast_to([P, 3, NT]), ALU.mult))
                    step(nc.vector.tensor_reduce(sf[:, :], hot[:, :, :], AX.X, ALU.add))
                    step(nc.vector.scalar_tensor_tensor(sf2[:, :], uf[:, :], float(UE), sf[:, :], ALU.mult, ALU.add))
                    step(nc.vector.tensor_scalar(sf2[:, :], sf2[:, :], float(E), None, ALU.min))
                    nc.vector.tensor_copy(unit_t[:, :, 0], sf2[:, :])
                    nc.vector.tensor_copy(unit_t[:, :, 1], jf[:, :]).then_inc(S("units_made"), 1)
                    v.wait_ge(S("ue_set"), 1)

                    def edge_scores(kk, slot, n):
                        v.wait_ge(S(f"ea_in{slot}"), n)
                        v.wait_ge(S("q_step"), kk * 2) if not isinstance(kk, int) else None
                        nc.vector.tensor_tensor(qp[:, :, :], ea_t[:, slot, :, :], ue_bc[:, :].unsqueeze(1).broadcast_to([EP, EB, AE]),
                                                ALU.mult).then_inc(S("ea_used"), 1)
                        v.wait_ge(S("ea_used"), kk + 1)
                        nc.vector.tensor_reduce(q_t[:, bass.ds(kk * EB, EB)], qp[:, :, :], AX.X, ALU.add).then_inc(S("q_step"), 2)

                    edge_scores(0, 0, 16)
                    with v.Fori(0, NE // 2) as h:
                        edge_scores(h * 2 + 1, 1, h * 16 + 16)
                        edge_scores(h * 2 + 2, 0, h * 16 + 32)
                    v.wait_ge(S("q_step"), 2 * NE)
                    v.sem_inc(S("q_made"), 1)

        def sqrt_stats():
            with nc.Block() as block:
                @block.scalar
                def _(act):
                    nc.scalar.activation(std[:, :], mv[:, :, 1], ACT.Sqrt, bias=eps_ln[0:TN, :]).then_inc(S("std"), 1)

                @block.vector
                def _(v):
                    v.wait_ge(S("std"), 1)
                    nc.vector.reciprocal(rstd[:, :], std[:, :])
            end_stage()

        def x_stats():
            with nc.Block() as block:
                @block.vector
                def _(v):
                    with v.Fori(0, NT // 2) as h:
                        for r in range(2):
                            nc.vector.bn_stats(stats[:, r, :], X[:, bass.ds(h * 2 + r, 1), :].rearrange("p o d -> p (o d)")).then_inc(S("stat"), 1)
                        for r in range(2):
                            v.wait_ge(S("stat"), h * 2 + (r + 1))
                            held(v, "stat_seen")
                            nc.vector.bn_aggr(aggr[:, r, :], stats[:, r, :]).then_inc(S("aggr"), 1)
                        for r in range(2):
                            v.wait_ge(S("aggr"), h * 2 + (r + 1))
                            copy(mv[:, bass.ds(h * 2 + r, 1), :].rearrange("p o d -> p (o d)"), aggr[:, r, :])
            sqrt_stats()

        end_stage()

        def node_rows(l, acc, sc):
            H = HEADS[l]
            DH = D // H
            W = DH + 1
            NW = H * W + H
            p = f"n{l}_"
            wext = sb(p + "wext", [P, 2, NW], F32, sc)
            wraw = sb(p + "wraw", [P, 2, D + AE], F32, sc)
            w2raw = sb(p + "w2raw", [P, 2, D], F32, sc)
            att = sb(p + "att", [P, 2, D], F32, sc)
            prod = sb(p + "prod", [P, 2, 2, D], F32, sc)
            xn = sb(p + "xn", [TN, 2, D], F32, sc)
            xnT = sb(p + "xnT", [P, 2, 2, TN], F32, sc)
            T = sb(p + "T", [TN, 2, NW], F32, sc)
            attc = sb(p + "attc", [P, 2, 1], F32, sc)
            attr = sb(p + "attr", [P, 2, 1], F32, sc)
            z = sb(p + "z", [TN, NT * H], F32, sc)

            with nc.Block() as block:
                @block.sync
                def _(sp):
                    if l == 0:
                        sp.dma_start(wraw[:, :, 0:D], a["L0_gnn_W"].rearrange("(k p) n -> p k n", p=P)).then_inc(S(p + "w"), 16)
                        for s, name in enumerate(("L0_gnn_att_src", "L0_gnn_att_dst")):
                            sp.dma_start(att[:, s, :], a[name].rearrange("(o h) d -> o (h d)", o=1).broadcast_to([P, D])).then_inc(S(p + "w"), 16)
                    else:
                        sp.dma_start(wraw[:, :, :], a["L1_gnn_W1"].rearrange("(k p) n -> p k n", p=P)).then_inc(S(p + "w"), 16)
                        sp.dma_start(w2raw[:, :, :], a["L1_gnn_W2"].rearrange("(k p) n -> p k n", p=P)).then_inc(S(p + "w"), 16)
                        sp.dma_start(attc[:, :, :], a["L1_gnn_att_l"].rearrange("z (o p) -> p o z", p=P), allow_slow_non_contiguous=True).then_inc(S(p + "w"), 16)
                        sp.dma_start(attr[:, :, :], a["L1_gnn_att_r"].rearrange("z (o p) -> p o z", p=P), allow_slow_non_contiguous=True).then_inc(S(p + "w"), 16)

                    def store(t, r, n):
                        after(sp, p + "T", n)
                        held(sp, p + "T_seen")
                        sp.dma_start(rows_d[l][bass.ds(t * TN, TN), :], T[:, r, 0:H * W]).then_inc(S(p + f"row_out{r}"), 16)

                    with sp.Fori(0, NT // 2) as h:
                        for r in range(2):
                            store(h * 2 + r, r, h * 2 + (r + 1))
                    for r in range(2):
                        sp.wait_ge(S(p + f"row_out{r}"), 16 * NT // 2 + 16)

                @block.tensor
                def _(pe):
                    if l == 1:
                        pe.wait_ge(S(p + "w"), 64)
                        for o in range(2):
                            for k in range(2):
                                mm = nc.tensor.transpose(bank[k][:, o * P:(o + 1) * P], w2raw[:, o, k * P:(k + 1) * P], ident[:, :])
                        for k in range(2):
                            for o in range(2):
                                mm = nc.tensor.matmul(bank[2 + k][:, 0:1], wraw[:, o, k * P:(k + 1) * P], attc[:, o, :],
                                                      start=(o == 0), stop=(o == 1))
                        mm.then_inc(S(p + "w2T"), 1)
                    pe.wait_ge(S(p + "wext"), 1)
                    with pe.Fori(0, NT // 2) as h:
                        for r in range(2):
                            t1 = h * 2 + (r + 1)
                            pe.wait_ge(S(p + "xn"), t1)
                            for k in range(2):
                                mm = nc.tensor.transpose(bank[4 + r][:, k * P:k * P + TN], xn[:, r, k * P:(k + 1) * P], ident[0:TN, 0:TN])
                            mm.then_inc(S(p + "xT"), 1)
                            pe.wait_ge(S(p + "xnT"), t1)
                            for k in range(2):
                                mm = nc.tensor.matmul(bank[6 + r][0:TN, 0:NW], xnT[:, r, k, :], wext[:, k, :], start=(k == 0), stop=(k == 1))
                            mm.then_inc(S(p + "row_mm"), 1)

                @block.scalar
                def _(act):
                    act.wait_ge(S(p + "xT"), 1)
                    with act.Fori(0, NT // 2) as h:
                        for r in range(2):
                            t1 = h * 2 + (r + 1)
                            act.wait_ge(S(p + "xT"), t1)
                            nc.scalar.copy(xnT[:, r, :, :], bank[4 + r][:, 0:2 * P].rearrange("p (k n) -> p k n", k=2)[:, :, 0:TN]).then_inc(S(p + "xnT"), 1)

                @block.vector
                def _(v):
                    if l == 0:
                        v.wait_ge(S(p + "w"), 48)
                        nc.vector.tensor_copy(wext[:, :, 0:H * W].rearrange("p k (h w) -> p k h w", h=H)[:, :, :, 0:DH],
                                              wraw[:, :, 0:D].rearrange("p k (h d) -> p k h d", h=H))
                        for s in range(2):
                            nc.vector.tensor_tensor(prod[:, s, :, :], wraw[:, :, 0:D], att[:, s, :].unsqueeze(1).broadcast_to([P, 2, D]), ALU.mult).then_inc(S(p + "prod"), 1)
                        v.wait_ge(S(p + "prod"), 2)
                        pv = prod[:, :, :, :].rearrange("p s k (h d) -> p s k h d", h=H)
                        for k in range(2):
                            nc.vector.tensor_reduce(wext[:, k, 0:H * W].rearrange("p (h w) -> p h w", h=H)[:, :, DH], pv[:, 0, k, :, :], AX.X, ALU.add)
                            ins = nc.vector.tensor_reduce(wext[:, k, H * W:NW], pv[:, 1, k, :, :], AX.X, ALU.add)
                        ins.then_inc(S(p + "wext"), 1)
                    else:
                        v.wait_ge(S(p + "w2T"), 1)
                        for k in range(2):
                            nc.vector.tensor_copy(wext[:, k, 0:D], bank[k][:, 0:D])
                            nc.vector.tensor_copy(wext[:, k, D:D + 1], bank[2 + k][:, 0:1])
                        nc.vector.tensor_copy(wext[:, :, D + 1:D + 2], attr[:, :, :]).then_inc(S(p + "wext"), 1)
                        nc.vector.memset(acc[:, :], 0.0)
                        nc.vector.memset(mrun[l][:, :], -BIG)
                    for r in range(2):
                        v.sem_inc(S(p + f"row_out{r}"), 16)
                    with v.Fori(0, NT // 2) as h:
                        for r in range(2):
                            t = h * 2 + r
                            nc.vector.tensor_scalar(xn[:, r, :], X[:, bass.ds(t, 1), :].rearrange("p o d -> p (o d)"), mv[:, bass.ds(t, 1), 0:1].rearrange("p o d -> p (o d)"), rstd[:, bass.ds(t, 1)],
                                                    ALU.subtract, ALU.mult).then_inc(S(p + "xn"), 1)
                            v.wait_ge(S(p + "row_mm"), t + 1)
                            v.wait_ge(S(p + f"row_out{r}"), h * 16 + 16)
                            nc.vector.tensor_copy(T[:, r, :], bank[6 + r][0:TN, 0:NW]).then_inc(S(p + "T"), 1)
                            v.wait_ge(S(p + "T"), t + 1)
                            copy(ad[l][:, bass.ds(t * H, H)], T[:, r, H * W:NW])
                            if l == 0:
                                copy(acc[:, bass.ds(t * H * W, H * W)], T[:, r, 0:H * W])
                                nc.vector.tensor_tensor(z[:, bass.ds(t * H, H)], T[:, r, 0:H * W].rearrange("p (h w) -> p h w", h=H)[:, :, DH],
                                                        T[:, r, H * W:NW], ALU.add)
                    if l == 0:
                        nc.vector.memset(stats[:, 0, :], 0.0).then_inc(S(p + "z"), 1)
                        v.wait_ge(S(p + "z"), 1)
                        nc.vector.scalar_tensor_tensor(mrun[l][:, :], z[:, :], SLOPES[l], z[:, :], ALU.mult, ALU.max)
                        nc.vector.memset(acc[:, :].rearrange("p (t w) -> p t w", w=W)[:, :, DH:W], 1.0)

        def attention(l, acc, sc):
            H = HEADS[l]
            DH = D // H
            W = DH + 1
            HW = H * W
            slope = SLOPES[l]
            p = f"g{l}_"
            pack = sb(p + "pack", [P, RING, Q, 2], I32, sc)
            drow = sb(p + "drow", [P, 2, 2, UE], F32, sc)
            qe = sb(p + "qe", [P, RING, Q], F32, sc)
            G = sb(p + "G", [P, RING, Q, HW], F32, sc)
            M = sb(p + "M", [P, RING, Q, TN], F32, sc)
            MT = sb(p + "MT", [TN, 2, 2, C, P], F32, sc)
            dloc = sb(p + "dloc", [P, 2, Q, H], F32, sc)
            b = sb(p + "b", [P, 2, Q, H], F32, sc)
            LT = sb(p + "LT", [Q * H, P], F32, sc)
            NEQ = sb(p + "NEQ", [Q * H, P + 1], F32, sc)
            FB = sb(p + "FB", [Q * H, P], F32, sc)
            RUN = sb(p + "RUN", [Q * H, P], F32, sc)
            SEL = sb(p + "SEL", [Q * H, P], F32, sc)
            RS = sb(p + "RS", [P, 2, Q, H], F32, sc)
            gone = sb(p + "gone", [TN, Q, H], F32, sc)
            top = sb(p + "top", [TN, Q, H], F32, sc)
            amax = sb(p + "amax", [TN, 2, H], F32, sc)
            zn = sb(p + "zn", [TN, 2, H], F32, sc)
            mloc = sb(p + "mloc", [TN, 2, H], F32, sc)
            rhs2 = sb(p + "rhs2", [TN, 2, 2, H], F32, sc)
            delta = sb(p + "delta", [TN, 2, H], F32, sc)
            c1 = sb(p + "c1", [TN, RING, 2, H], F32, sc)
            ze = sb(p + "ze", [P, Q, H], F32, sc)
            le = sb(p + "le", [P, Q, H], F32, sc)
            te = sb(p + "te", [P, Q, H], F32, sc)
            tm = sb(p + "tm", [P, 2, Q, H], F32, sc)
            QH = Q * H
            adl, mr = ad[l], mrun[l]

            def slots(slot):
                for i in range(RING):
                    slot(i, i)
                yield
                for i in range(SU + LAG - RING, SU + LAG):
                    slot(i, i % RING)
                yield

            def run(eng, slot):
                peeled = slots(slot)
                next(peeled)
                with eng.Fori(0, BODIES - 2) as it:
                    for r in range(RING):
                        slot(it * RING + (RING + r), r)
                next(peeled)

            def has(i, lag):
                return not isinstance(i, int) or lag <= i < SU + lag

            def filled(i, r, n):
                if isinstance(i, int):
                    return (i // RING + 1) * n
                return (i - r) * (n // RING) + n

            with nc.Block() as block:
                @block.sync
                def _(sp):
                    def slot(i, r):
                        if not has(i, 0):
                            return
                        if not isinstance(i, int) or i >= RING:
                            after(sp, p + f"rows_in{r}", filled(i - RING, r, 16 * Q))
                            held(sp, p + "rows_seen")
                            after(sp, p + "dloc", i - (RING - 1))
                            held(sp, p + "dloc_seen")
                        if not isinstance(i, int) or i >= 2:
                            after(sp, p + "MT", i - 1)
                            held(sp, p + "MT_seen")
                        if l == 1 and (not isinstance(i, int) or i >= RING):
                            after(sp, p + "b", i - (RING - 1))
                        held(sp, p + "slot_seen")
                        for u in range(2):
                            s = sp.value_load(unit_i[0:1, bass.ds(i * 4 + 2 * u, 1)], min_val=0, max_val=E)
                            sp.dma_start(pack[:, r, u * C:(u + 1) * C, :],
                                         pack_d[bass.ds(s, UE), :].rearrange("(p c) k -> p c k", p=P)).then_inc(S(p + f"pack_in{r}"), 16)
                            sp.dma_start(drow[:, r % 2, u, :],
                                         dst_d[bass.ds(s, UE)].rearrange("(o e) -> o e", o=1).broadcast_to([P, UE])).then_inc(S(p + f"drow_in{r}"), 16)
                            if l == 1:
                                sp.dma_start(qe[:, r, u * C:(u + 1) * C],
                                             q_d[bass.ds(s, UE)].rearrange("(p c) -> p c", p=P)).then_inc(S(p + f"q_in{r}"), 16)
                    run(sp, slot)

                @block.gpsimd
                def _(pool):
                    def slot(i, r):
                        if not has(i, 0):
                            return
                        pool.wait_ge(S(p + f"pack_in{r}"), filled(i, r, 32))
                        if not isinstance(i, int) or i >= RING:
                            after(pool, p + "summed", i - (RING - 1))
                        held(pool, p + "pool_seen")
                        for q in range(Q):
                            nc.gpsimd.indirect_dma_start(G[:, r, q, :], None, rows_d[l],
                                                         bass.IndirectOffsetOnAxis(ap=pack[:, r, q, 0:1], axis=0)).then_inc(S(p + f"rows_in{r}"), 16)
                    run(pool, slot)

                @block.tensor
                def _(pe):
                    def slot(i, r):
                        r1, r2 = (r - 1) % RING, (r - 2) % RING
                        if has(i, 1):
                            pe.wait_ge(S(p + "SEL"), i)
                            held(pe, p + "sel_seen")
                            nc.tensor.transpose(bank[1][:, 0:QH], SEL[:, :], ident[0:QH, 0:QH])
                            nc.tensor.transpose(bank[1][:, QH:2 * QH], NEQ[:, 1:P + 1], ident[0:QH, 0:QH]).then_inc(S(p + "selT"), 1)
                        if has(i, 0):
                            pe.wait_ge(S(p + "b"), i + 1)
                            nc.tensor.transpose(bank[0][0:QH, 0:P], b[:, r % 2, :, :].rearrange("p q h -> p (q h)"), ident[:, :])
                            nc.tensor.transpose(bank[0][0:QH, P:2 * P], dloc[:, r % 2, :, :].rearrange("p q h -> p (q h)"), ident[:, :]).then_inc(S(p + "rowT"), 1)
                        if has(i, 1):
                            pe.wait_ge(S(p + "RS"), i)
                            for q in range(Q):
                                mm = nc.tensor.matmul(bank[2][0:TN, q * 2 * H:(q + 1) * 2 * H], M[:, r1, q, :], RS[:, :, q, :], start=True, stop=True)
                            mm.then_inc(S(p + "V"), 1)
                            pe.wait_ge(S(p + "rhs2"), i)
                            if not isinstance(i, int) or i >= 2:
                                after(pe, p + "te", i - 1)
                            for q in range(Q):
                                mm = nc.tensor.matmul(bank[3][:, q * 2 * H:(q + 1) * 2 * H], MT[:, r1 % 2, q // C, q % C, :],
                                                      rhs2[:, q // C, :, :], start=True, stop=True)
                            mm.then_inc(S(p + "Xe"), 1)
                        if has(i, 2):
                            pe.wait_ge(S(p + "scaled"), i - 1)
                            if not isinstance(i, int) or i >= 4:
                                after(pe, p + "merged", i - 3)
                            for q in range(Q):
                                mm = nc.tensor.matmul(bank[4 + 2 * (r2 % 2) + q // C][0:TN, 0:HW], M[:, r2, q, :], G[:, r2, q, :],
                                                      start=(q % C == 0), stop=(q % C == C - 1))
                            mm.then_inc(S(p + "summed"), 1)
                    run(pe, slot)

                @block.scalar
                def _(act):
                    def slot(i, r):
                        r1 = (r - 1) % RING
                        if has(i, 1):
                            act.wait_ge(S(p + "selT"), i)
                            if not isinstance(i, int) or i >= 2:
                                after(act, p + "V", i - 1)
                            nc.scalar.copy(RS[:, :, :, :].rearrange("p k q h -> p (k q h)"), bank[1][:, 0:2 * QH]).then_inc(S(p + "RS"), 1)
                        if has(i, 0):
                            act.wait_ge(S(p + "rowT"), i + 1)
                            if not isinstance(i, int) or i >= 1:
                                after(act, p + "NEQ", i)
                            nc.scalar.copy(LT[:, :], bank[0][0:QH, P:2 * P]).then_inc(S(p + "LT"), 1)
                        if has(i, 1):
                            act.wait_ge(S(p + "delta"), i)
                            if not isinstance(i, int) or i >= RING:
                                after(act, p + "merged", i - (RING - 1))
                            nc.scalar.activation(c1[:, r1, :, :], delta[:, :, :], ACT.Exp).then_inc(S(p + "c1"), 1)
                            act.wait_ge(S(p + "tm"), i)
                            nc.scalar.activation(G[:, r1, :, :].rearrange("p q (h w) -> p q h w", h=H)[:, :, :, DH], tm[:, r1 % 2, :, :],
                                                 ACT.Exp).then_inc(S(p + "w"), 1)
                    run(act, slot)

                @block.vector
                def _(v):
                    nc.vector.memset(NEQ[:, :], 1.0).then_inc(S(p + "NEQ_set"), 1)
                    v.wait_ge(S(p + "NEQ_set"), 1)

                    def tile_of(i, u):
                        return v.value_load(unit_i[0:1, bass.ds(i * 4 + (2 * u + 1), 1)], min_val=0, max_val=NT - 1)

                    def slot(i, r):
                        r1, r2, r3 = (r - 1) % RING, (r - 2) % RING, (r - 3) % RING
                        one, cur, two, three = has(i, 1), has(i, 0), has(i, 2), has(i, 3)
                        jc = [tile_of(i, u) for u in range(2)] if cur else None
                        if one:
                            v.wait_ge(S(p + "LT"), i)
                            if not isinstance(i, int) or i >= 2:
                                after(v, p + "selT", i - 1)
                            nc.vector.tensor_tensor(NEQ[:, 1:P], LT[:, 1:P], LT[:, 0:P - 1], ALU.not_equal).then_inc(S(p + "NEQ"), 1)
                        if cur:
                            v.wait_ge(S(p + f"pack_in{r}"), filled(i, r, 32))
                            if not isinstance(i, int) or i >= 2:
                                after(v, p + "rowT", i - 1)
                            for u in range(2):
                                ins = nc.vector.tensor_scalar(dloc[:, r % 2, u * C:(u + 1) * C, :],
                                                              pack[:, r, u * C:(u + 1) * C, 1:2].bitcast(F32).broadcast_to([P, C, H]),
                                                              base[:, bass.ds(jc[u], 1)], None, ALU.subtract)
                            ins.then_inc(S(p + "dloc"), 1)
                        if one:
                            v.wait_ge(S(p + "NEQ"), i)
                            nc.vector.tensor_scalar(FB[:, :], NEQ[:, 0:P], -BIG, None, ALU.mult).then_inc(S(p + "FB"), 1)
                        if cur:
                            v.wait_ge(S(p + f"drow_in{r}"), filled(i, r, 32))
                            if not isinstance(i, int) or i >= 2:
                                after(v, p + "Xe", i - 1)
                            nc.vector.tensor_scalar(MT[:, r % 2, 0, :, :], drow[0:TN, r % 2, 0, :].rearrange("p (e c) -> p c e", c=C),
                                                    nid[0:TN, bass.ds(jc[0], 1)], None, ALU.is_equal)
                        if one:
                            v.wait_ge(S(p + "FB"), i)
                            nc.vector.tensor_tensor_scan(RUN[:, :], FB[:, :], bank[0][0:QH, 0:P], 0.0, ALU.add, ALU.max).then_inc(S(p + "RUN"), 1)
                        if cur:
                            nc.vector.tensor_scalar(MT[:, r % 2, 1, :, :], drow[0:TN, r % 2, 1, :].rearrange("p (e c) -> p c e", c=C),
                                                    nid[0:TN, bass.ds(jc[1], 1)], None, ALU.is_equal).then_inc(S(p + "MT"), 1)
                        if one:
                            v.wait_ge(S(p + "RUN"), i)
                            nc.vector.tensor_tensor(SEL[:, :], RUN[:, :], NEQ[:, 1:P + 1], ALU.mult).then_inc(S(p + "SEL"), 1)
                        if cur:
                            v.wait_ge(S(p + f"rows_in{r}"), filled(i, r, 16 * Q))
                            src_part = G[:, r, :, :].rearrange("p q (h w) -> p q h w", h=H)[:, :, :, DH]
                            if l == 0:
                                nc.vector.tensor_copy(b[:, r % 2, :, :], src_part).then_inc(S(p + "b"), 1)
                            else:
                                v.wait_ge(S(p + f"q_in{r}"), filled(i, r, 32))
                                nc.vector.tensor_tensor(b[:, r % 2, :, :], src_part, qe[:, r, :].unsqueeze(2), ALU.add).then_inc(S(p + "b"), 1)
                            v.wait_ge(S(p + "dloc"), i + 1)
                            nc.vector.tensor_tensor(M[:, r, :, :], iota_n[:, :].unsqueeze(1).broadcast_to([P, Q, TN]),
                                                    dloc[:, r % 2, :, 0:1].broadcast_to([P, Q, TN]), ALU.is_equal).then_inc(S(p + "M"), 1)
                        jm = [tile_of(i - 3, u) for u in range(2)] if three else None

                        def merge(u):
                            if not three:
                                return
                            at = acc[:, bass.ds(jm[u] * HW, HW)]
                            if u == 0:
                                v.wait_ge(S(p + "summed"), i - 2)
                                v.wait_ge(S(p + "c1"), i - 2)
                            if u == 1 or not isinstance(i, int) or i >= 4:
                                after(v, p + "acc", (i - 3) * 2 + u)
                            a3 = at.rearrange("p (h w) -> p h w", h=H)
                            nc.vector.tensor_tensor(a3, a3, c1[:, r3, u, :].unsqueeze(2).broadcast_to([TN, H, W]), ALU.mult).then_inc(S(p + "acc_c"), 1)
                            return at

                        def add(u, at):
                            if not three:
                                return
                            v.wait_ge(S(p + "acc_c"), (i - 3) * 2 + (u + 1))
                            ins = nc.vector.tensor_tensor(at, at, bank[4 + 2 * (r3 % 2) + u][0:TN, 0:HW], ALU.add)
                            ins.then_inc(S(p + "acc"), 1)

                        if one:
                            jn = [tile_of(i - 1, u) for u in range(2)]
                            V = bank[2][0:TN, 0:2 * QH].rearrange("p (q k h) -> p q k h", k=2, h=H)
                            if not isinstance(i, int) or i >= 2:
                                after(v, p + "Xe", i - 1)
                            for u in range(2):
                                copy(rhs2[:, u, 0, :], adl[:, bass.ds(jn[u] * H, H)])
                        at0 = merge(0)
                        if one:
                            v.wait_ge(S(p + "V"), i)
                            nc.vector.tensor_scalar(gone[:, :, :], V[:, :, 1, :], -1.0, BIG, ALU.add, ALU.mult).then_inc(S(p + "gone"), 1)
                        add(0, at0)
                        if one:
                            v.wait_ge(S(p + "gone"), i)
                            nc.vector.tensor_tensor(top[:, :, :], gone[:, :, :], V[:, :, 0, :], ALU.add).then_inc(S(p + "top"), 1)
                        at1 = merge(1)
                        if one:
                            v.wait_ge(S(p + "top"), i)
                            nc.vector.tensor_reduce(amax[:, :, :], top[:, :, :].rearrange("p (u c) h -> p u h c", u=2), AX.X, ALU.max).then_inc(S(p + "amax"), 1)
                        add(1, at1)
                        if three:
                            v.wait_ge(S(p + "acc"), (i - 3) * 2 + 2)
                            v.sem_inc(S(p + "merged"), 1)
                        if one:
                            v.wait_ge(S(p + "amax"), i)
                            nc.vector.tensor_tensor(zn[:, :, :], amax[:, :, :], rhs2[:, :, 0, :], ALU.add).then_inc(S(p + "zn"), 1)
                            v.wait_ge(S(p + "zn"), i)
                            nc.vector.scalar_tensor_tensor(mloc[:, :, :], zn[:, :, :], slope, zn[:, :, :], ALU.mult, ALU.max).then_inc(S(p + "mloc"), 1)
                            v.wait_ge(S(p + "mloc"), i)
                            if not isinstance(i, int) or i >= 2:
                                after(v, p + "c1", i - 1)
                            for u in range(2):
                                m_at = mr[:, bass.ds(jn[u] * H, H)]
                                if u == 1 or not isinstance(i, int) or i >= 2:
                                    after(v, p + "mrun", (i - 1) * 2 + u)
                                nc.vector.tensor_tensor(rhs2[:, u, 1, :], mloc[:, u, :], m_at, ALU.max).then_inc(S(p + "mnew"), 1)
                                v.wait_ge(S(p + "mnew"), (i - 1) * 2 + (u + 1))
                                nc.vector.tensor_tensor(delta[:, u, :], m_at, rhs2[:, u, 1, :], ALU.subtract).then_inc(S(p + "delta_u"), 1)
                                v.wait_ge(S(p + "delta_u"), (i - 1) * 2 + (u + 1))
                                copy(m_at, rhs2[:, u, 1, :]).then_inc(S(p + "mrun"), 1)
                            v.wait_ge(S(p + "mrun"), (i - 1) * 2 + 2)
                            v.sem_inc(S(p + "rhs2"), 1)
                            v.sem_inc(S(p + "delta"), 1)

                        def scale(k):
                            if not two:
                                return
                            if k == 0:
                                v.wait_ge(S(p + "w"), i - 1)
                            g = G[:, r2, 2 * k:2 * k + 2, :].rearrange("p q (h w) -> p (q h) w", h=H)
                            ins = nc.vector.tensor_tensor(g[:, :, 0:DH], g[:, :, 0:DH], g[:, :, DH:W].broadcast_to([P, 2 * H, DH]), ALU.mult)
                            if k == 3:
                                ins.then_inc(S(p + "scaled"), 1)

                        scale(0)
                        scale(1)
                        XE = bank[3][:, 0:2 * QH].rearrange("p (q k h) -> p q k h", k=2, h=H)
                        if one:
                            v.wait_ge(S(p + "Xe"), i)
                            nc.vector.tensor_tensor(ze[:, :, :], b[:, r1 % 2, :, :], XE[:, :, 0, :], ALU.add).then_inc(S(p + "ze"), 1)
                        scale(2)
                        if one:
                            v.wait_ge(S(p + "ze"), i)
                            nc.vector.scalar_tensor_tensor(le[:, :, :], ze[:, :, :], slope, ze[:, :, :], ALU.mult, ALU.max).then_inc(S(p + "le"), 1)
                        scale(3)
                        if one:
                            v.wait_ge(S(p + "le"), i)
                            nc.vector.tensor_tensor(te[:, :, :], le[:, :, :], XE[:, :, 1, :], ALU.subtract).then_inc(S(p + "te"), 1)
                            v.wait_ge(S(p + "te"), i)
                            if not isinstance(i, int) or i >= 3:
                                after(v, p + "w", i - 2)
                            nc.vector.tensor_scalar(tm[:, r1 % 2, :, :], te[:, :, :], 0.0, None, ALU.min).then_inc(S(p + "tm"), 1)

                    run(v, slot)

        def finish_attention(l, acc, sc):
            H = HEADS[l]
            DH = D // H
            W = DH + 1
            HW = H * W
            p = f"f{l}_"
            bias = sb(p + "bias", [TN, D], F32, sc)
            den = sb(p + "den", [TN, NT * H], F32, sc)
            y = sb(p + "y", [TN, 2, D], F32, sc)
            with nc.Block() as block:
                @block.sync
                def _(sp):
                    sp.dma_start(bias[:, :], a[f"L{l}_gnn_bias"].rearrange("(o d) -> o d", o=1).broadcast_to([TN, D])).then_inc(S(p + "bias"), 16)

                @block.vector
                def _(v):
                    nc.vector.tensor_scalar(den[:, :], acc[:, :].rearrange("p (t w) -> p t w", w=W)[:, :, DH], 1e-30, None, ALU.max).then_inc(S(p + "den"), 1)
                    v.wait_ge(S(p + "den"), 1)
                    nc.vector.reciprocal(den[:, :], den[:, :]).then_inc(S(p + "den"), 1)
                    v.wait_ge(S(p + "den"), 2)
                    v.wait_ge(S(p + "bias"), 16)
                    with v.Fori(0, NT // 2) as h:
                        for r in range(2):
                            t = h * 2 + r
                            nc.vector.tensor_tensor(y[:, r, :].rearrange("p (h w) -> p h w", h=H),
                                                    acc[:, bass.ds(t * HW, HW)].rearrange("p (h w) -> p h w", h=H)[:, :, 0:DH],
                                                    den[:, bass.ds(t * H, H)].unsqueeze(2).broadcast_to([TN, H, DH]), ALU.mult)
                            nc.vector.tensor_tensor(X[:, bass.ds(t, 1), :].rearrange("p o d -> p (o d)"), X[:, bass.ds(t, 1), :].rearrange("p o d -> p (o d)"),
                                                    bias[:, :], ALU.add).then_inc(S(p + "y"), 1)
                        for r in range(2):
                            t = h * 2 + r
                            xt = X[:, bass.ds(t, 1), :].rearrange("p o d -> p (o d)")
                            v.wait_ge(S(p + "y"), h * 2 + 2)
                            nc.vector.tensor_tensor(xt, xt, y[:, r, :], ALU.add).then_inc(S(p + "x"), 1)
                        for r in range(2):
                            t = h * 2 + r
                            v.wait_ge(S(p + "x"), h * 2 + (r + 1))
                            held(v, p + "x_seen")
                            nc.vector.bn_stats(stats[:, r, :], X[:, bass.ds(t, 1), :].rearrange("p o d -> p (o d)")).then_inc(S(p + "s"), 1)
                        for r in range(2):
                            v.wait_ge(S(p + "s"), h * 2 + (r + 1))
                            held(v, p + "s_seen")
                            nc.vector.bn_aggr(aggr[:, r, :], stats[:, r, :]).then_inc(S(p + "aggr"), 1)
                        for r in range(2):
                            v.wait_ge(S(p + "aggr"), h * 2 + (r + 1))
                            copy(mv[:, bass.ds(h * 2 + r, 1), :].rearrange("p o d -> p (o d)"), aggr[:, r, :])

        def experts(l, sc):
            NX = EXPERTS[l]
            p = f"e{l}_"
            wr = sb(p + "wr", [P, 2, P if l == 0 else NX], F32, sc)
            wr2 = sb(p + "wr2", [P, NX], F32, sc)
            br1 = sb(p + "br1", [P, 1], F32, sc)
            br = sb(p + "br", [TN, NX], F32, sc)
            w1 = sb(p + "w1", [P, 2, NX, D], F32, sc)
            w2 = sb(p + "w2", [P, 2, NX, D], F32, sc)
            w3 = sb(p + "w3", [P, 2, NX, D], F32, sc)
            bo = sb(p + "bo", [NX, D], F32, sc)
            NQ = (2, 10)[l]
            names = (("L0_ffn_expert_b1", "L0_ffn_expert_b2"),
                     tuple("L1_ffn_" + n for n in ("b1", "g1", "be1", "m1", "v1", "b2", "g2", "be2", "m2", "v2")))[l]
            tab_r = sb(p + "tab_r", [NQ * NX, D], F32, sc)
            tab = sb(p + "tab", [P, 2, NQ, NX], F32, sc)
            sc_c = sb(p + "sc_c", [P, 2, 2, NX], F32, sc)
            bi_c = sb(p + "bi_c", [P, 2, 2, NX], F32, sc)
            before = sb(p + "before", [TN, NX, NX], F32, sc)
            xn = sb(p + "xn", [TN, GT, D], F32, sc)
            xnT = sb(p + "xnT", [P, 2, 2, GN], F32, sc)
            rhT = sb(p + "rhT", [P, GN], F32, sc)
            lg = sb(p + "lg", [TN, GT, NX], F32, sc)
            lmax = sb(p + "lmax", [TN, GT, 1], F32, sc)
            ex = sb(p + "ex", [TN, GT, NX], F32, sc)
            es = sb(p + "es", [TN, GT, 1], F32, sc)
            gt = sb(p + "gt", [TN, GT, NX, NX], F32, sc)
            eq = sb(p + "eq", [TN, GT, NX, NX], F32, sc)
            rank = sb(p + "rank", [TN, GT, NX], F32, sc)
            cw = sb(p + "cw", [TN, 2, GT, NX], F32, sc)
            cwT = sb(p + "cwT", [NX, GT, TN], F32, sc)
            h1 = sb(p + "h1", [P, 2, GN], F32, sc)
            h2 = sb(p + "h2", [P, 2, 2, GN], F32, sc)
            NXT = NG + 1
            wn = (("L0_ffn_expert_w1", "L0_ffn_expert_w2", "L0_ffn_expert_w3"), ("L1_ffn_W1", "L1_ffn_W2", "L1_ffn_Wo"))[l]
            out_v = out.rearrange("(t p) d -> p t d", p=TN)
            NGATE = 12

            def run(eng, slot):
                slot(0, 0)
                slot(1, 1)
                with eng.Fori(0, (NXT - 4) // 2) as it:
                    for r in range(2):
                        slot(it * 2 + (2 + r), r)
                slot(NXT - 2, 0)
                slot(NXT - 1, 1)

            def isprep(i):
                return not isinstance(i, int) or i < NG

            def isexp(i):
                return not isinstance(i, int) or i >= 1

            def col(name):
                return a[name].rearrange("e (k p) -> p e k", p=P)

            with nc.Block() as block:
                @block.sync
                def _(sp):
                    n = 0
                    for w, name in zip((w1, w2, w3), wn):
                        for k in range(2):
                            sp.dma_start(w[:, k, :, :], a[name][:, k * P:(k + 1) * P, :].rearrange("e p n -> p e n")).then_inc(S(p + "w"), 16)
                    if l == 0:
                        sp.dma_start(bo[:, :], a["L0_ffn_expert_b3"]).then_inc(S(p + "w"), 16)
                    else:
                        sp.dma_start(bo[:, :], a["L1_ffn_bo"]).then_inc(S(p + "w"), 16)
                        def flush(i, r):
                            if isexp(i):
                                sp.wait_ge(S(p + "group"), i)
                                held(sp, p + "group_seen")
                                sp.dma_start(out_v[:, bass.ds((i - 1) * GT, GT), :], X[:, bass.ds((i - 1) * GT, GT), :]).then_inc(S("out_done"), 16)
                        run(sp, flush)
                        sp.wait_ge(S("out_done"), 16 * NG)

                @block.gpsimd
                def _(pool):
                    nc.gpsimd.memset(before[:, :, :], 1.0).then_inc(S(p + "before"), 1)
                    pool.wait_ge(S(p + "before"), 1)
                    nc.gpsimd.affine_select(out=before[:, :, :], in_=before[:, :, :], compare_op=ALU.is_gt, fill=0.0, base=0,
                                            pattern=[[1, NX], [-1, NX]], channel_multiplier=0).then_inc(S(p + "before"), 1)

                @block.tensor
                def _(pe):
                    pe.wait_ge(S(p + "w"), 16 * 7)
                    pe.wait_ge(S(p + "sw"), 16 * (NQ + (4, 2)[l]))
                    for k in range(2):
                        mm = nc.tensor.transpose(bank[0][:, k * P:k * P + NQ * NX], tab_r[:, k * P:(k + 1) * P], ident[0:NQ * NX, 0:NQ * NX])
                    mm.then_inc(S(p + "tab_mm"), 1)
                    pe.wait_ge(S(p + "small"), 1)

                    def slot(i, r):
                        g = 1 - r

                        def prep(k):
                            if not isprep(i):
                                return
                            if k == 0:
                                pe.wait_ge(S(p + "xn"), i + 1)
                                if not isinstance(i, int) or i >= 1:
                                    after(pe, p + "b3", i)
                                for u in range(GT):
                                    for kk in range(2):
                                        mm = nc.tensor.transpose(bank[6][:, kk * 256 + u * TN:kk * 256 + (u + 1) * TN], xn[:, u, kk * P:(kk + 1) * P],
                                                                 ident[0:TN, 0:TN])
                                mm.then_inc(S(p + "xT"), 1)
                            if k == 1:
                                pe.wait_ge(S(p + "xnT"), i + 1)
                                if l == 0:
                                    for kk in range(2):
                                        mm = nc.tensor.matmul(bank[7][:, 0:GN], wr[:, kk, :], xnT[:, r, kk, :], start=(kk == 0), stop=(kk == 1))
                                    mm.then_inc(S(p + "rh_mm"), 1)
                            if k == 2:
                                if l == 0:
                                    pe.wait_ge(S(p + "rhT"), i + 1)
                                    for u in range(GT):
                                        mm = nc.tensor.matmul(bank[7][0:TN, 256 + u * 16:256 + u * 16 + NX], rhT[:, u * TN:(u + 1) * TN], wr2[:, :],
                                                              start=True, stop=True)
                                else:
                                    for u in range(GT):
                                        for kk in range(2):
                                            mm = nc.tensor.matmul(bank[7][0:TN, 256 + u * 16:256 + u * 16 + NX], xnT[:, r, kk, u * TN:(u + 1) * TN],
                                                                  wr[:, kk, :], start=(kk == 0), stop=(kk == 1))
                                mm.then_inc(S(p + "lg_mm"), 1)
                            if k == 4:
                                pe.wait_ge(S(p + "cw"), i + 1)
                                for u in range(GT):
                                    mm = nc.tensor.transpose(bank[7][0:NX, u * P:u * P + TN], cw[:, r, u, :], ident[0:TN, 0:TN])
                                mm.then_inc(S(p + "cwT_mm"), 1)
                            if k == 5:
                                pe.wait_ge(S(p + "cwT"), i + 1)
                                for u in range(GT):
                                    mm = nc.tensor.matmul(bank[6][0:TN, u * 256:u * 256 + D], cwT[:, u, :], bo[:, :], start=True, stop=True)
                                mm.then_inc(S(p + "b3_mm"), 1)

                        def layer1(e):
                            if not isexp(i):
                                return
                            if e or not isinstance(i, int) or i >= 2:
                                after(pe, p + "h1", (i - 1) * NX + e)
                            for m in range(2):
                                for kk in range(2):
                                    mm = nc.tensor.matmul(bank[m][:, 0:GN], w1[:, kk, e, m * P:(m + 1) * P], xnT[:, g, kk, :], start=(kk == 0), stop=(kk == 1))
                            mm.then_inc(S(p + "h1_mm"), 1)

                        def layer2(e):
                            if not isexp(i):
                                return
                            pe.wait_ge(S(p + "h1"), (i - 1) * NX + (e + 1))
                            if e or not isinstance(i, int) or i >= 2:
                                after(pe, p + "h2", (i - 1) * NX + e)
                            for m in range(2):
                                for kk in range(2):
                                    mm = nc.tensor.matmul(bank[2 + m][:, 0:GN], w2[:, kk, e, m * P:(m + 1) * P], h1[:, kk, :], start=(kk == 0), stop=(kk == 1))
                            mm.then_inc(S(p + "h2_mm"), 1)

                        def layer3(e):
                            if not isexp(i):
                                return
                            pe.wait_ge(S(p + "h2"), (i - 1) * NX + (e + 1))
                            if e or not isinstance(i, int) or i >= 2:
                                after(pe, p + "o", (i - 1) * NX + e)
                            for u in range(GT):
                                for kk in range(2):
                                    mm = nc.tensor.matmul(bank[4 + u][0:TN, 0:D], h2[:, e % 2, kk, u * TN:(u + 1) * TN], w3[:, kk, e, :],
                                                          start=(kk == 0), stop=(kk == 1))
                            mm.then_inc(S(p + "o_mm"), 1)

                        prep(0)
                        for e in range(NX + 1):
                            if e == 0:
                                layer1(0)
                            else:
                                layer2(e - 1)
                                if e < NX:
                                    layer1(e)
                                layer3(e - 1)
                            prep(e + 1)
                    run(pe, slot)

                @block.scalar
                def _(act):
                    if l == 0:
                        act.dma_start(wr[:, :, :], a["L0_ffn_router_w1"].rearrange("(k p) n -> p k n", p=P)).then_inc(S(p + "sw"), 16)
                        act.dma_start(wr2[:, :], a["L0_ffn_router_w2"]).then_inc(S(p + "sw"), 16)
                        act.dma_start(br1[:, :], a["L0_ffn_router_b1"].rearrange("(p o) -> p o", o=1), allow_slow_non_contiguous=True).then_inc(S(p + "sw"), 16)
                        act.dma_start(br[:, :], a["L0_ffn_router_b2"].rearrange("(o n) -> o n", o=1).broadcast_to([TN, NX])).then_inc(S(p + "sw"), 16)
                        nsw = 16 * (4 + NQ)
                    else:
                        act.dma_start(wr[:, :, :], a["L1_ffn_Wr"].rearrange("(k p) n -> p k n", p=P)).then_inc(S(p + "sw"), 16)
                        act.dma_start(br[:, :], a["L1_ffn_br"].rearrange("(o n) -> o n", o=1).broadcast_to([TN, NX])).then_inc(S(p + "sw"), 16)
                        nsw = 16 * (2 + NQ)
                    for q, nm in enumerate(names):
                        act.dma_start(tab_r[q * NX:(q + 1) * NX, :], a[nm]).then_inc(S(p + "sw"), 16)
                    act.wait_ge(S(p + "sw"), nsw)
                    act.wait_ge(S(p + "tab_mm"), 1)
                    nc.scalar.copy(tab[:, :, :, :].rearrange("p k q e -> p k (q e)"),
                                   bank[0][:, 0:2 * P].rearrange("p (k n) -> p k n", k=2)[:, :, 0:NQ * NX]).then_inc(S(p + "tab"), 1)
                    act.wait_ge(S(p + "tab"), 1)
                    if l == 1:
                        for q in range(2):
                            ins = nc.scalar.activation(sc_c[:, q, :, :], tab[:, :, 5 * q + 4, :], ACT.Sqrt, bias=eps_bn[:, :])
                        ins.then_inc(S(p + "bn_std"), 1)
                    act.wait_ge(S(p + "small"), 1)

                    def slot(i, r):
                        def prep(k):
                            if not isprep(i):
                                return
                            if k == 0:
                                act.wait_ge(S(p + "xT"), i + 1)
                                nc.scalar.copy(xnT[:, r, :, :], bank[6][:, :].rearrange("p (k n) -> p k n", k=2)[:, :, 0:GN]).then_inc(S(p + "xnT"), 1)
                            if k == 2 and l == 0:
                                act.wait_ge(S(p + "rh_mm"), i + 1)
                                nc.scalar.activation(rhT[:, :], bank[7][:, 0:GN], ACT.Relu, bias=br1[:, :]).then_inc(S(p + "rhT"), 1)
                            if k == 3:
                                act.wait_ge(S(p + "gate"), i * NGATE + 3)
                                nc.scalar.activation(ex[:, :, :], lg[:, :, :], ACT.Exp).then_inc(S(p + "ex"), 1)
                                if l == 0:
                                    act.wait_ge(S(p + "gate"), i * NGATE + NGATE)
                                    nc.scalar.activation(ex[:, :, :], lg[:, :, :], ACT.Exp).then_inc(S(p + "ex2"), 1)
                            if k == 5:
                                act.wait_ge(S(p + "cwT_mm"), i + 1)
                                nc.scalar.copy(cwT[:, :, :], bank[7][0:NX, 0:2 * P].rearrange("p (u n) -> p u n", u=GT)[:, :, 0:TN]).then_inc(S(p + "cwT"), 1)

                        def relu(e, q):
                            if not isexp(i):
                                return
                            dst = h1 if q == 0 else h2[:, e % 2, :, :]
                            act.wait_ge(S(p + f"h{q + 1}_mm"), (i - 1) * NX + (e + 1))
                            if q == 0 and (e or not isinstance(i, int) or i >= 2):
                                after(act, p + "h2_mm", (i - 1) * NX + e)
                            if q == 1 and (e >= 2 or not isinstance(i, int) or i >= 2):
                                after(act, p + "o_mm", (i - 1) * NX + (e - 1))
                            for m in range(2):
                                if l == 0:
                                    ins = nc.scalar.activation(dst[:, m, :], bank[2 * q + m][:, 0:GN], ACT.Relu, bias=tab[:, m, q, e:e + 1])
                                else:
                                    ins = nc.scalar.activation(dst[:, m, :], bank[2 * q + m][:, 0:GN], ACT.Relu, bias=bi_c[:, q, m, e:e + 1],
                                                               scale=sc_c[:, q, m, e:e + 1])
                            ins.then_inc(S(p + f"h{q + 1}"), 1)

                        prep(0)
                        for e in range(NX + 1):
                            if e == 0:
                                relu(0, 0)
                            else:
                                relu(e - 1, 1)
                                if e < NX:
                                    relu(e, 0)
                            prep(e + 1)
                    run(act, slot)

                @block.vector
                def _(v):
                    if l == 1:
                        v.wait_ge(S(p + "bn_std"), 1)
                        k = [0]

                        def step(ins):
                            k[0] += 1
                            ins.then_inc(S(p + "bn"), 1)
                            v.wait_ge(S(p + "bn"), k[0])

                        for q in range(2):
                            o = 5 * q
                            step(nc.vector.reciprocal(sc_c[:, q, :, :], sc_c[:, q, :, :]))
                            step(nc.vector.tensor_tensor(sc_c[:, q, :, :], sc_c[:, q, :, :], tab[:, :, o + 1, :], ALU.mult))
                            step(nc.vector.tensor_tensor(bi_c[:, q, :, :], tab[:, :, o, :], tab[:, :, o + 3, :], ALU.subtract))
                            step(nc.vector.tensor_tensor(bi_c[:, q, :, :], bi_c[:, q, :, :], sc_c[:, q, :, :], ALU.mult))
                            step(nc.vector.tensor_tensor(bi_c[:, q, :, :], bi_c[:, q, :, :], tab[:, :, o + 2, :], ALU.add))
                    v.wait_ge(S(p + "sw"), 16 * (NQ + (4, 2)[l]))
                    v.wait_ge(S(p + "tab"), 1)
                    v.wait_ge(S(p + "before"), 2)
                    v.sem_inc(S(p + "small"), 1)

                    def xtile(t):
                        return X[:, bass.ds(t, 1), :].rearrange("p o d -> p (o d)")

                    def slot(i, r):
                        g = 1 - r
                        n = [0]

                        def gate(ins):
                            n[0] += 1
                            ins.then_inc(S(p + "gate"), 1)
                            v.wait_ge(S(p + "gate"), i * NGATE + n[0])

                        def prep(k):
                            if not isprep(i):
                                return
                            if k == 0:
                                if not isinstance(i, int) or i >= 1:
                                    after(v, p + "xT", i)
                                for u in range(GT):
                                    t = i * GT + u
                                    ins = nc.vector.tensor_scalar(xn[:, u, :], xtile(t), mv[:, bass.ds(t, 1), 0:1].rearrange("p o d -> p (o d)"),
                                                                  rstd[:, bass.ds(t, 1)], ALU.subtract, ALU.mult)
                                ins.then_inc(S(p + "xn"), 1)
                            if k == 3:
                                v.wait_ge(S(p + "lg_mm"), i + 1)
                                L = bank[7][0:TN, 256:256 + 16 * GT].rearrange("p (u n) -> p u n", u=GT)[:, :, 0:NX]
                                gate(nc.vector.tensor_tensor(lg[:, :, :], L, br[:, :].unsqueeze(1).broadcast_to([TN, GT, NX]), ALU.add))
                                gate(nc.vector.tensor_reduce(lmax[:, :, 0], lg[:, :, :], AX.X, ALU.max))
                                gate(nc.vector.tensor_tensor(lg[:, :, :], lg[:, :, :], lmax[:, :, :].broadcast_to([TN, GT, NX]), ALU.subtract))
                                v.wait_ge(S(p + "ex"), i + 1)
                                gate(nc.vector.tensor_reduce(es[:, :, 0], ex[:, :, :], AX.X, ALU.add))
                                gate(nc.vector.reciprocal(es[:, :, :], es[:, :, :]))
                                if l == 1:
                                    after(v, p + "o", (i - 1) * NX) if not isinstance(i, int) or i >= 2 else None
                                    nc.vector.tensor_tensor(cw[:, r, :, :], ex[:, :, :], es[:, :, :].broadcast_to([TN, GT, NX]), ALU.mult).then_inc(S(p + "cw"), 1)
                                    for _ in range(NGATE - 5):
                                        n[0] += 1
                                    v.sem_inc(S(p + "gate"), NGATE - 5)
                                else:
                                    gate(nc.vector.tensor_tensor(ex[:, :, :], ex[:, :, :], es[:, :, :].broadcast_to([TN, GT, NX]), ALU.mult))
                                    for u in range(GT):
                                        pe_, pf_ = ex[:, u, :].unsqueeze(2).broadcast_to([TN, NX, NX]), ex[:, u, :].unsqueeze(1).broadcast_to([TN, NX, NX])
                                        nc.vector.tensor_tensor(gt[:, u, :, :], pf_, pe_, ALU.is_gt)
                                        ins = nc.vector.tensor_tensor(eq[:, u, :, :], pf_, pe_, ALU.is_equal)
                                    gate(ins)
                                    gate(nc.vector.tensor_tensor(eq[:, :, :, :], eq[:, :, :, :], before[:, :, :].unsqueeze(1).broadcast_to([TN, GT, NX, NX]), ALU.mult))
                                    gate(nc.vector.tensor_tensor(gt[:, :, :, :], gt[:, :, :, :], eq[:, :, :, :], ALU.add))
                                    gate(nc.vector.tensor_reduce(rank[:, :, :], gt[:, :, :, :], AX.X, ALU.add))
                                    gate(nc.vector.tensor_reduce(lmax[:, :, 0], ex[:, :, :], AX.X, ALU.max))
                                    gate(nc.vector.tensor_tensor(lg[:, :, :], ex[:, :, :], lmax[:, :, :].broadcast_to([TN, GT, NX]), ALU.subtract))
                            if k == 4 and l == 0:
                                v.wait_ge(S(p + "ex2"), i + 1)
                                nc.vector.scalar_tensor_tensor(lg[:, :, :], rank[:, :, :], 1.5, ex[:, :, :], ALU.is_lt, ALU.mult).then_inc(S(p + "g2"), 1)
                                v.wait_ge(S(p + "g2"), i * 3 + 1)
                                nc.vector.tensor_reduce(es[:, :, 0], lg[:, :, :], AX.X, ALU.add).then_inc(S(p + "g2"), 1)
                                v.wait_ge(S(p + "g2"), i * 3 + 2)
                                nc.vector.reciprocal(es[:, :, :], es[:, :, :]).then_inc(S(p + "g2"), 1)
                                v.wait_ge(S(p + "g2"), i * 3 + 3)
                                nc.vector.tensor_tensor(cw[:, r, :, :], lg[:, :, :], es[:, :, :].broadcast_to([TN, GT, NX]), ALU.mult).then_inc(S(p + "cw"), 1)
                            if k == 6:
                                v.wait_ge(S(p + "b3_mm"), i + 1)
                                for u in range(GT):
                                    xt = xtile(i * GT + u)
                                    ins = nc.vector.tensor_tensor(xt, xt, bank[6][0:TN, u * 256:u * 256 + D], ALU.add)
                                ins.then_inc(S(p + "b3"), 1)

                        def collect(e):
                            if not isexp(i):
                                return
                            v.wait_ge(S(p + "o_mm"), (i - 1) * NX + (e + 1))
                            if e == 0:
                                v.wait_ge(S(p + "b3"), i)
                            else:
                                v.wait_ge(S(p + "o"), (i - 1) * NX + e)
                            for u in range(GT):
                                xt = xtile((i - 1) * GT + u)
                                ins = nc.vector.scalar_tensor_tensor(xt, bank[4 + u][0:TN, 0:D], cw[:, g, u, e:e + 1], xt, ALU.mult, ALU.add)
                            ins.then_inc(S(p + "o"), 1)

                        prep(0)
                        for e in range(NX + 1):
                            if e >= 1:
                                collect(e - 1)
                            prep(e + 1)
                        if isexp(i):
                            v.wait_ge(S(p + "o"), (i - 1) * NX + NX)
                            v.sem_inc(S(p + "group"), 1)
                    run(v, slot)

        for l in (0, 1):
            x_stats()
            with ExitStack() as s1:
                acc = sb(f"acc{l}", [TN, NT * HEADS[l] * (D // HEADS[l] + 1)], F32, s1)
                for part in (node_rows, attention, finish_attention):
                    with ExitStack() as s2:
                        part(l, acc, s2)
                    end_stage()
            sqrt_stats()
            with ExitStack() as s1:
                experts(l, s1)
            end_stage()


def kernel(**inputs):
    import concourse.bacc as bacc
    from concourse.bass_utils import run_bass_kernel_spmd

    nc = bacc.Bacc("TRN2", target_bir_lowering=False, num_devices=1)
    arrays, aps = {}, {}
    for name in inputs:
        v = np.ascontiguousarray(inputs[name])
        arrays[f"in_{name}"] = v
        aps[name] = nc.dram_tensor(f"in_{name}", v.shape, mybir.dt.from_np(v.dtype), kind="ExternalInput").ap()
    out = nc.dram_tensor("out_x", (N, D), F32, kind="ExternalOutput").ap()
    build(nc, aps, out)
    r = run_bass_kernel_spmd(nc, [arrays], core_ids=[0])
    return r.results[0]["out_x"]
```

```python
from contextlib import ExitStack

import numpy as np
import concourse.bass as bass
from concourse import mybir

F32 = mybir.dt.float32
I32 = mybir.dt.int32
BF16 = mybir.dt.bfloat16
ALU = mybir.AluOpType
ACT = mybir.ActivationFunctionType
AX = mybir.AxisListType

P = 128
N = 6250
D = 256
TN = 125
NT = N // TN
E = 106250
EP = 125
EC = E // EP
C = 4
UE = P * C
UNITS = (E + (UE - 1) * NT) // UE
SU = (UNITS + 1) // 2
Q = 2 * C
LOG_UE = 9
EPAD = E + UE
AE = 64
RING = 4
LAG = 3
BODIES = (SU + LAG) // RING
GT = 2
GN = GT * TN
NG = NT // GT
BIG = 1.0e30
LN_EPS = 1e-5
BN_EPS = 1e-3
assert UE == 1 << LOG_UE and (SU + LAG) % RING == 0 and (NG + 1) % 2 == 0 and EP * EC == E

HEADS = (4, 1)
SLOPES = (0.2, 0.01)
EXPERTS = (6, 8)


def build(nc, a, out):
    ctx = ExitStack()
    with ctx:
        def sb(name, shape, dt=F32, scope=ctx):
            return scope.enter_context(nc.sbuf_tensor(name, shape, dt))

        sems = {}
        stage = [0]

        def S(name):
            if name not in sems:
                sems[name] = nc.alloc_semaphore(name=f"{name}_{stage[0]}")
            return sems[name]

        def end_stage():
            nc.clear_and_free_semaphores(list(sems.values()))
            sems.clear()
            stage[0] += 1
            nc.all_engine_barrier()

        def after(eng, name, count):
            if not isinstance(count, int) or count > 0:
                eng.wait_ge(S(name), count)

        def held(eng, name):
            eng.sem_inc(S(name), 1)

        def copy(out_, in_):
            return nc.vector.tensor_scalar(out_, in_, 1.0, None, ALU.mult)

        bank = [ctx.enter_context(nc.psum_tensor(f"bank{k}", [P, 512], F32)) for k in range(8)]

        pack_d = nc.dram_tensor("edge_pack", [EPAD, 2], I32).ap()
        dst_d = nc.dram_tensor("edge_dst", [2, EPAD], BF16).ap()
        ubase_d = nc.dram_tensor("unit_base", [3 * P], F32).ap()
        q_d = nc.dram_tensor("edge_q", [EPAD], F32).ap()
        unit_d = nc.dram_tensor("unit_table", [3 * P, 2], I32).ap()
        rows_d = [nc.dram_tensor(f"rows{l}", [N, HEADS[l] * (D // HEADS[l] + 1)], F32).ap() for l in (0, 1)]

        X = sb("X", [TN, NT, D])
        ident = sb("ident", [P, P])
        iota_n = sb("iota_n", [P, TN])
        iota_b = sb("iota_b", [P, TN], BF16)
        nid = sb("nid", [P, NT])
        base = sb("base", [P, NT])
        ones = sb("ones", [P, P])
        unit_i = sb("unit_i", [1, 6 * P], I32)
        ubase = sb("ubase", [P, 3 * P])
        unit_j = sb("unit_j", [1, 3 * P], I32)
        unode = sb("unode", [P, 3 * P])
        ones_bf = sb("ones_bf", [2, TN], BF16)
        eps_ln = sb("eps_ln", [P, 1])
        eps_bn = sb("eps_bn", [P, 1])
        stats = sb("stats", [TN, 2, 6])
        aggr = sb("aggr", [TN, 2, 2])
        mv = sb("mv", [TN, NT, 2])
        std = sb("std", [TN, NT])
        rstd = sb("rstd", [TN, NT])
        ad = [sb(f"ad{l}", [TN, NT * HEADS[l]]) for l in (0, 1)]
        mrun = [sb(f"mrun{l}", [TN, NT * HEADS[l]]) for l in (0, 1)]
        ue_bc = sb("ue_bc", [EP, AE])

        with ExitStack() as sc:
            src_t = sb("src_t", [EP, EC], I32, sc)
            dst_t = sb("dst_t", [EP, EC], I32, sc)
            dstf = sb("dstf", [EP, EC], F32, sc)
            pack_t = sb("pack_t", [EP, EC, 2], I32, sc)
            pad_pack = sb("pad_pack", [P, C, 2], I32, sc)
            pad_hl = sb("pad_hl", [P, 2, C], BF16, sc)
            lo_i = sb("lo_i", [EP, EC], I32, sc)
            hl = sb("hl", [EP, 2, EC], BF16, sc)
            ub = sb("ub", [P, 3], F32, sc)
            pad_q = sb("pad_q", [P, C], F32, sc)
            below = sb("below", [EP, EC], F32, sc)
            cnt = sb("cnt", [EP, NT + 1], F32, sc)
            int_n = sb("int_n", [P, TN], I32, sc)
            int_nid = sb("int_nid", [P, NT], I32, sc)
            int_base = sb("int_base", [P, NT], I32, sc)
            int_u = sb("int_u", [P, 3], I32, sc)
            uf = sb("uf", [P, 3], F32, sc)
            tile_f = sb("tile_f", [P, NT], F32, sc)
            int_tile = sb("int_tile", [P, NT], I32, sc)
            bound = sb("bound", [P, NT], F32, sc)
            zeros = sb("zeros", [P, NT], F32, sc)
            ptr = sb("ptr", [P, NT + 1], F32, sc)
            wide = sb("wide", [P, NT], F32, sc)
            wide_i = sb("wide_i", [P, NT], I32, sc)
            nunit_i = sb("nunit_i", [P, NT], I32, sc)
            nunit = sb("nunit", [P, NT], F32, sc)
            ends = sb("ends", [P, NT], F32, sc)
            starts = sb("starts", [P, NT], F32, sc)
            off = sb("off", [P, NT], F32, sc)
            ge = sb("ge", [P, 3, NT], F32, sc)
            jf = sb("jf", [P, 3], F32, sc)
            hot = sb("hot", [P, 3, NT], F32, sc)
            sf = sb("sf", [P, 3], F32, sc)
            sf2 = sb("sf2", [P, 3], F32, sc)
            unit_t = sb("unit_t", [P, 3, 2], I32, sc)
            w1a = sb("w1a", [P, 2, AE], F32, sc)
            attl = sb("attl", [P, 2, 1], F32, sc)
            attl_b = sb("attl_b", [P, 2, EP], F32, sc)
            EB = 34
            NE = EC // EB
            assert NE * EB == EC and NE % 2 == 1
            ea_t = sb("ea_t", [EP, 2, EB, AE], F32, sc)
            qp = sb("qp", [EP, EB, AE], F32, sc)
            q_t = sb("q_t", [EP, EC], F32, sc)
            ea_v = a["edge_attr_64"].rearrange("(p c) f -> p c f", p=EP)

            with nc.Block() as block:
                @block.sync
                def _(sp):
                    sp.dma_start(src_t[:, :], a["src"].rearrange("(p c) -> p c", p=EP)).then_inc(S("src_in"), 16)
                    sp.dma_start(dst_t[:, :], a["dst"].rearrange("(p c) -> p c", p=EP)).then_inc(S("dst_in"), 16)
                    sp.dma_start(X[:, :, :], a["x"].rearrange("(t p) d -> p t d", p=TN)).then_inc(S("x_in"), 16)
                    sp.wait_ge(S("pads_set"), 1)
                    sp.dma_start(pack_d[E:EPAD, :].rearrange("(p c) k -> p c k", p=P), pad_pack[:, :, :]).then_inc(S("pad_out"), 16)
                    sp.dma_start(dst_d[:, E:EPAD].rearrange("k (p c) -> p k c", p=P), pad_hl[:, :, :]).then_inc(S("pad_out"), 16)
                    sp.dma_start(q_d[E:EPAD].rearrange("(p c) -> p c", p=P), pad_q[:, :]).then_inc(S("pad_out"), 16)
                    sp.wait_ge(S("pack_made"), 1)
                    sp.dma_start(pack_d[0:E, :].rearrange("(p c) k -> p c k", p=EP), pack_t[:, :, :]).then_inc(S("pack_out"), 16)
                    sp.dma_start(dst_d[:, 0:E].rearrange("k (p c) -> p k c", p=EP), hl[:, :, :]).then_inc(S("pack_out"), 16)
                    sp.wait_ge(S("units_made"), 1)
                    sp.dma_start(unit_d.rearrange("(p k) t -> p k t", p=P), unit_t[:, :, :]).then_inc(S("unit_out"), 16)
                    sp.dma_start(ubase_d.rearrange("(p k) -> p k", p=P), ub[:, :]).then_inc(S("unit_out"), 16)
                    sp.wait_ge(S("unit_out"), 32)
                    sp.dma_start(ubase[:, :], ubase_d.rearrange("(o u) -> o u", o=1).broadcast_to([P, 3 * P])).then_inc(S("ubase_in"), 16)
                    sp.dma_start(unit_j[:, :], unit_d.rearrange("(o u) t -> o u t", o=1)[:, :, 1], allow_slow_non_contiguous=True).then_inc(S("unit_in"), 16)
                    sp.dma_start(unit_i[:, :], unit_d.rearrange("(o u) t -> o (u t)", o=1)).then_inc(S("unit_in"), 16)
                    sp.wait_ge(S("q_made"), 1)
                    sp.dma_start(q_d[0:E].rearrange("(p c) -> p c", p=EP), q_t[:, :]).then_inc(S("q_out"), 16)
                    sp.wait_ge(S("pad_out"), 48)
                    sp.wait_ge(S("pack_out"), 32)
                    sp.wait_ge(S("unit_in"), 32)
                    sp.wait_ge(S("q_out"), 16)
                    sp.wait_ge(S("x_in"), 16)

                @block.gpsimd
                def _(pool):
                    nc.gpsimd.memset(ident[:, :], 0.0).then_inc(S("ident_zero"), 1)
                    pool.wait_ge(S("ident_zero"), 1)
                    nc.gpsimd.affine_select(out=ident[:, :], in_=ident[:, :], compare_op=ALU.not_equal, fill=1.0,
                                            base=0, pattern=[[-1, P]], channel_multiplier=1).then_inc(S("ident_set"), 1)
                    nc.gpsimd.iota(int_n[:, :], pattern=[[1, TN]], base=0, channel_multiplier=0)
                    nc.gpsimd.iota(int_nid[:, :], pattern=[[TN, NT]], base=0, channel_multiplier=1)
                    nc.gpsimd.iota(int_base[:, :], pattern=[[TN, NT]], base=0, channel_multiplier=0)
                    nc.gpsimd.iota(int_tile[:, :], pattern=[[1, NT]], base=0, channel_multiplier=0)
                    nc.gpsimd.iota(int_u[:, :], pattern=[[1, 3]], base=0, channel_multiplier=3).then_inc(S("iotas"), 1)
                    nc.gpsimd.memset(ones[:, :], 1.0)
                    nc.gpsimd.memset(zeros[:, :], 0.0)
                    nc.gpsimd.memset(eps_ln[:, :], LN_EPS)
                    nc.gpsimd.memset(eps_bn[:, :], BN_EPS)
                    nc.gpsimd.memset(cnt[:, :], 0.0).then_inc(S("fills"), 1)
                    nc.gpsimd.memset(pad_hl[:, 0, :], -1.0)
                    nc.gpsimd.memset(pad_hl[:, 1, :], 0.0)
                    nc.gpsimd.memset(ones_bf[:, :], 1.0)
                    nc.gpsimd.memset(pad_q[:, :], 0.0)
                    nc.gpsimd.memset(pad_pack[:, :, 0:1], 0)
                    nc.gpsimd.memset(pad_pack[:, :, 1:2].bitcast(F32), -1.0).then_inc(S("pads_set"), 1)

                @block.scalar
                def _(act):
                    act.dma_start(w1a[:, :, :], a["L1_gnn_W1"][:, D:D + AE].rearrange("(o p) f -> p o f", p=P)).then_inc(S("ue_in"), 16)
                    act.dma_start(attl[:, :, :], a["L1_gnn_att_l"].rearrange("z (o p) -> p o z", p=P), allow_slow_non_contiguous=True).then_inc(S("ue_in"), 16)
                    act.wait_ge(S("ue_mm"), 1)
                    nc.scalar.copy(ue_bc[:, :], bank[1][0:EP, 0:AE]).then_inc(S("ue_set"), 1)

                    def load_ea(k, slot):
                        act.dma_start(ea_t[:, slot, :, :], ea_v[:, bass.ds(k * EB, EB), :]).then_inc(S(f"ea_in{slot}"), 16)

                    load_ea(0, 0)
                    with act.Fori(0, NE // 2) as h:
                        load_ea(h * 2 + 1, 1)
                        act.wait_ge(S("ea_used"), h * 2 + 1)
                        load_ea(h * 2 + 2, 0)
                        act.wait_ge(S("ea_used"), h * 2 + 2)

                @block.tensor
                def _(pe):
                    pe.wait_ge(S("fills"), 1)
                    pe.wait_ge(S("counts"), 1)
                    nc.tensor.matmul(bank[0][:, 0:NT + 1], ones[0:EP, :], cnt[:, :], start=True, stop=True).then_inc(S("ptr_mm"), 1)
                    pe.wait_ge(S("attl_b"), 1)
                    for o in range(2):
                        mm = nc.tensor.matmul(bank[1][0:EP, 0:AE], attl_b[:, o, :], w1a[:, o, :], start=(o == 0), stop=(o == 1))
                    mm.then_inc(S("ue_mm"), 1)

                @block.vector
                def _(v):
                    v.wait_ge(S("iotas"), 1)
                    nc.vector.tensor_copy(iota_n[:, :], int_n[:, :])
                    nc.vector.tensor_copy(iota_b[:, :], int_n[:, :])
                    nc.vector.tensor_copy(nid[:, :], int_nid[:, :])
                    nc.vector.tensor_copy(base[:, :], int_base[:, :]).then_inc(S("consts"), 1)
                    nc.vector.tensor_copy(uf[:, :], int_u[:, :])
                    nc.vector.tensor_copy(tile_f[:, :], int_tile[:, :])
                    v.wait_ge(S("consts"), 1)
                    nc.vector.tensor_scalar(bound[:, :], base[:, :], float(TN), None, ALU.add).then_inc(S("bound"), 1)
                    v.wait_ge(S("fills"), 1)
                    v.wait_ge(S("ue_in"), 32)
                    nc.vector.tensor_copy(attl_b[:, :, :], attl[:, :, :].broadcast_to([P, 2, EP])).then_inc(S("attl_b"), 1)
                    v.wait_ge(S("dst_in"), 16)
                    v.wait_ge(S("src_in"), 16)
                    nc.vector.tensor_copy(dstf[:, :], dst_t[:, :]).then_inc(S("dstf"), 1)
                    nc.vector.tensor_copy(pack_t[:, :, 0], src_t[:, :])
                    v.wait_ge(S("dstf"), 1)
                    nc.vector.tensor_copy(pack_t[:, :, 1].bitcast(F32), dstf[:, :])
                    nc.vector.tensor_scalar(lo_i[:, :], dst_t[:, :], P - 1, None, ALU.bitwise_and).then_inc(S("lo"), 1)
                    v.wait_ge(S("lo"), 1)
                    nc.vector.tensor_copy(hl[:, 1, :], lo_i[:, :])
                    nc.vector.tensor_tensor(hl[:, 0, :], dst_t[:, :], lo_i[:, :], ALU.subtract).then_inc(S("pack_made"), 1)
                    v.wait_ge(S("bound"), 1)
                    with v.Fori(0, NT) as t:
                        v.wait_ge(S("bound"), t + 1)
                        nc.vector.tensor_scalar(below[:, :], dstf[:, :], bound[0:EP, bass.ds(t, 1)], 0.0, ALU.is_lt, ALU.add,
                                                accum_out=cnt[:, bass.ds(t + 1, 1)]).then_inc(S("bound"), 1)
                    v.wait_ge(S("bound"), NT + 1)
                    v.sem_inc(S("counts"), 1)
                    v.wait_ge(S("ptr_mm"), 1)
                    k = [0]

                    def step(ins):
                        k[0] += 1
                        ins.then_inc(S("unit_step"), 1)
                        v.wait_ge(S("unit_step"), k[0])

                    step(nc.vector.tensor_copy(ptr[:, :], bank[0][:, 0:NT + 1]))
                    step(nc.vector.tensor_tensor(wide[:, :], ptr[:, 1:NT + 1], ptr[:, 0:NT], ALU.subtract))
                    step(nc.vector.tensor_scalar(wide_i[:, :], wide[:, :], float(UE - 1), None, ALU.add))
                    step(nc.vector.tensor_scalar(nunit_i[:, :], wide_i[:, :], LOG_UE, None, ALU.arith_shift_right))
                    step(nc.vector.tensor_copy(nunit[:, :], nunit_i[:, :]))
                    step(nc.vector.tensor_tensor_scan(ends[:, :], nunit[:, :], zeros[:, :], 0.0, ALU.add, ALU.add))
                    step(nc.vector.tensor_tensor(starts[:, :], ends[:, :], nunit[:, :], ALU.subtract))
                    step(nc.vector.scalar_tensor_tensor(off[:, :], starts[:, :], -float(UE), ptr[:, 0:NT], ALU.mult, ALU.add))
                    step(nc.vector.tensor_tensor(ge[:, :, :], uf[:, :].unsqueeze(2).broadcast_to([P, 3, NT]),
                                                 ends[:, :].unsqueeze(1).broadcast_to([P, 3, NT]), ALU.is_ge))
                    step(nc.vector.tensor_reduce(jf[:, :], ge[:, :, :], AX.X, ALU.add))
                    step(nc.vector.tensor_scalar(jf[:, :], jf[:, :], float(NT - 1), None, ALU.min))
                    step(nc.vector.tensor_tensor(hot[:, :, :], jf[:, :].unsqueeze(2).broadcast_to([P, 3, NT]),
                                                 tile_f[:, :].unsqueeze(1).broadcast_to([P, 3, NT]), ALU.is_equal))
                    step(nc.vector.tensor_tensor(hot[:, :, :], hot[:, :, :], off[:, :].unsqueeze(1).broadcast_to([P, 3, NT]), ALU.mult))
                    step(nc.vector.tensor_reduce(sf[:, :], hot[:, :, :], AX.X, ALU.add))
                    step(nc.vector.scalar_tensor_tensor(sf2[:, :], uf[:, :], float(UE), sf[:, :], ALU.mult, ALU.add))
                    step(nc.vector.tensor_scalar(sf2[:, :], sf2[:, :], float(E), None, ALU.min))
                    nc.vector.tensor_scalar(ub[:, :], jf[:, :], float(TN), None, ALU.mult)
                    nc.vector.tensor_copy(unit_t[:, :, 0], sf2[:, :])
                    nc.vector.tensor_copy(unit_t[:, :, 1], jf[:, :]).then_inc(S("units_made"), 1)
                    v.wait_ge(S("ubase_in"), 16)
                    nc.vector.tensor_scalar(unode[:, :], ubase[:, :], nid[:, 0:1], -1.0, ALU.add, ALU.mult)
                    v.wait_ge(S("ue_set"), 1)

                    def edge_scores(kk, slot, n):
                        v.wait_ge(S(f"ea_in{slot}"), n)
                        v.wait_ge(S("q_step"), kk * 2) if not isinstance(kk, int) else None
                        nc.vector.tensor_tensor(qp[:, :, :], ea_t[:, slot, :, :], ue_bc[:, :].unsqueeze(1).broadcast_to([EP, EB, AE]),
                                                ALU.mult).then_inc(S("ea_used"), 1)
                        v.wait_ge(S("ea_used"), kk + 1)
                        nc.vector.tensor_reduce(q_t[:, bass.ds(kk * EB, EB)], qp[:, :, :], AX.X, ALU.add).then_inc(S("q_step"), 2)

                    edge_scores(0, 0, 16)
                    with v.Fori(0, NE // 2) as h:
                        edge_scores(h * 2 + 1, 1, h * 16 + 16)
                        edge_scores(h * 2 + 2, 0, h * 16 + 32)
                    v.wait_ge(S("q_step"), 2 * NE)
                    v.sem_inc(S("q_made"), 1)

        def sqrt_stats():
            with nc.Block() as block:
                @block.scalar
                def _(act):
                    nc.scalar.activation(std[:, :], mv[:, :, 1], ACT.Sqrt, bias=eps_ln[0:TN, :]).then_inc(S("std"), 1)

                @block.vector
                def _(v):
                    v.wait_ge(S("std"), 1)
                    nc.vector.reciprocal(rstd[:, :], std[:, :])
            end_stage()

        def x_stats():
            with nc.Block() as block:
                @block.vector
                def _(v):
                    with v.Fori(0, NT // 2) as h:
                        for r in range(2):
                            nc.vector.bn_stats(stats[:, r, :], X[:, bass.ds(h * 2 + r, 1), :].rearrange("p o d -> p (o d)")).then_inc(S("stat"), 1)
                        for r in range(2):
                            v.wait_ge(S("stat"), h * 2 + (r + 1))
                            held(v, "stat_seen")
                            nc.vector.bn_aggr(aggr[:, r, :], stats[:, r, :]).then_inc(S("aggr"), 1)
                        for r in range(2):
                            v.wait_ge(S("aggr"), h * 2 + (r + 1))
                            copy(mv[:, bass.ds(h * 2 + r, 1), :].rearrange("p o d -> p (o d)"), aggr[:, r, :])
            sqrt_stats()

        end_stage()

        def node_rows(l, acc, sc):
            H = HEADS[l]
            DH = D // H
            W = DH + 1
            NW = H * W + H
            p = f"n{l}_"
            wext = sb(p + "wext", [P, 2, NW], F32, sc)
            wraw = sb(p + "wraw", [P, 2, D + AE], F32, sc)
            w2raw = sb(p + "w2raw", [P, 2, D], F32, sc)
            att = sb(p + "att", [P, 2, D], F32, sc)
            prod = sb(p + "prod", [P, 2, 2, D], F32, sc)
            xn = sb(p + "xn", [TN, 2, D], F32, sc)
            xnT = sb(p + "xnT", [P, 2, 2, TN], F32, sc)
            T = sb(p + "T", [TN, 2, NW], F32, sc)
            attc = sb(p + "attc", [P, 2, 1], F32, sc)
            attr = sb(p + "attr", [P, 2, 1], F32, sc)
            z = sb(p + "z", [TN, NT * H], F32, sc)

            with nc.Block() as block:
                @block.sync
                def _(sp):
                    if l == 0:
                        sp.dma_start(wraw[:, :, 0:D], a["L0_gnn_W"].rearrange("(k p) n -> p k n", p=P)).then_inc(S(p + "w"), 16)
                        for s, name in enumerate(("L0_gnn_att_src", "L0_gnn_att_dst")):
                            sp.dma_start(att[:, s, :], a[name].rearrange("(o h) d -> o (h d)", o=1).broadcast_to([P, D])).then_inc(S(p + "w"), 16)
                    else:
                        sp.dma_start(wraw[:, :, :], a["L1_gnn_W1"].rearrange("(k p) n -> p k n", p=P)).then_inc(S(p + "w"), 16)
                        sp.dma_start(w2raw[:, :, :], a["L1_gnn_W2"].rearrange("(k p) n -> p k n", p=P)).then_inc(S(p + "w"), 16)
                        sp.dma_start(attc[:, :, :], a["L1_gnn_att_l"].rearrange("z (o p) -> p o z", p=P), allow_slow_non_contiguous=True).then_inc(S(p + "w"), 16)
                        sp.dma_start(attr[:, :, :], a["L1_gnn_att_r"].rearrange("z (o p) -> p o z", p=P), allow_slow_non_contiguous=True).then_inc(S(p + "w"), 16)

                    def store(t, r, n):
                        after(sp, p + "T", n)
                        held(sp, p + "T_seen")
                        sp.dma_start(rows_d[l][bass.ds(t * TN, TN), :], T[:, r, 0:H * W]).then_inc(S(p + f"row_out{r}"), 16)

                    with sp.Fori(0, NT // 2) as h:
                        for r in range(2):
                            store(h * 2 + r, r, h * 2 + (r + 1))
                    for r in range(2):
                        sp.wait_ge(S(p + f"row_out{r}"), 16 * NT // 2 + 16)

                @block.tensor
                def _(pe):
                    if l == 1:
                        pe.wait_ge(S(p + "w"), 64)
                        for o in range(2):
                            for k in range(2):
                                mm = nc.tensor.transpose(bank[k][:, o * P:(o + 1) * P], w2raw[:, o, k * P:(k + 1) * P], ident[:, :])
                        for k in range(2):
                            for o in range(2):
                                mm = nc.tensor.matmul(bank[2 + k][:, 0:1], wraw[:, o, k * P:(k + 1) * P], attc[:, o, :],
                                                      start=(o == 0), stop=(o == 1))
                        mm.then_inc(S(p + "w2T"), 1)
                    pe.wait_ge(S(p + "wext"), 1)
                    with pe.Fori(0, NT // 2) as h:
                        for r in range(2):
                            t1 = h * 2 + (r + 1)
                            pe.wait_ge(S(p + "xn"), t1)
                            for k in range(2):
                                mm = nc.tensor.transpose(bank[4 + r][:, k * P:k * P + TN], xn[:, r, k * P:(k + 1) * P], ident[0:TN, 0:TN])
                            mm.then_inc(S(p + "xT"), 1)
                            pe.wait_ge(S(p + "xnT"), t1)
                            for k in range(2):
                                mm = nc.tensor.matmul(bank[6 + r][0:TN, 0:NW], xnT[:, r, k, :], wext[:, k, :], start=(k == 0), stop=(k == 1))
                            mm.then_inc(S(p + "row_mm"), 1)

                @block.scalar
                def _(act):
                    act.wait_ge(S(p + "xT"), 1)
                    with act.Fori(0, NT // 2) as h:
                        for r in range(2):
                            t1 = h * 2 + (r + 1)
                            act.wait_ge(S(p + "xT"), t1)
                            nc.scalar.copy(xnT[:, r, :, :], bank[4 + r][:, 0:2 * P].rearrange("p (k n) -> p k n", k=2)[:, :, 0:TN]).then_inc(S(p + "xnT"), 1)

                @block.vector
                def _(v):
                    if l == 0:
                        v.wait_ge(S(p + "w"), 48)
                        nc.vector.tensor_copy(wext[:, :, 0:H * W].rearrange("p k (h w) -> p k h w", h=H)[:, :, :, 0:DH],
                                              wraw[:, :, 0:D].rearrange("p k (h d) -> p k h d", h=H))
                        for s in range(2):
                            nc.vector.tensor_tensor(prod[:, s, :, :], wraw[:, :, 0:D], att[:, s, :].unsqueeze(1).broadcast_to([P, 2, D]), ALU.mult).then_inc(S(p + "prod"), 1)
                        v.wait_ge(S(p + "prod"), 2)
                        pv = prod[:, :, :, :].rearrange("p s k (h d) -> p s k h d", h=H)
                        for k in range(2):
                            nc.vector.tensor_reduce(wext[:, k, 0:H * W].rearrange("p (h w) -> p h w", h=H)[:, :, DH], pv[:, 0, k, :, :], AX.X, ALU.add)
                            ins = nc.vector.tensor_reduce(wext[:, k, H * W:NW], pv[:, 1, k, :, :], AX.X, ALU.add)
                        ins.then_inc(S(p + "wext"), 1)
                    else:
                        v.wait_ge(S(p + "w2T"), 1)
                        for k in range(2):
                            nc.vector.tensor_copy(wext[:, k, 0:D], bank[k][:, 0:D])
                            nc.vector.tensor_copy(wext[:, k, D:D + 1], bank[2 + k][:, 0:1])
                        nc.vector.tensor_copy(wext[:, :, D + 1:D + 2], attr[:, :, :]).then_inc(S(p + "wext"), 1)
                        nc.vector.memset(acc[:, :], 0.0)
                        nc.vector.memset(mrun[l][:, :], -BIG)
                    for r in range(2):
                        v.sem_inc(S(p + f"row_out{r}"), 16)
                    with v.Fori(0, NT // 2) as h:
                        for r in range(2):
                            t = h * 2 + r
                            nc.vector.tensor_scalar(xn[:, r, :], X[:, bass.ds(t, 1), :].rearrange("p o d -> p (o d)"), mv[:, bass.ds(t, 1), 0:1].rearrange("p o d -> p (o d)"), rstd[:, bass.ds(t, 1)],
                                                    ALU.subtract, ALU.mult).then_inc(S(p + "xn"), 1)
                            v.wait_ge(S(p + "row_mm"), t + 1)
                            v.wait_ge(S(p + f"row_out{r}"), h * 16 + 16)
                            nc.vector.tensor_copy(T[:, r, :], bank[6 + r][0:TN, 0:NW]).then_inc(S(p + "T"), 1)
                            v.wait_ge(S(p + "T"), t + 1)
                            copy(ad[l][:, bass.ds(t * H, H)], T[:, r, H * W:NW])
                            if l == 0:
                                copy(acc[:, bass.ds(t * H * W, H * W)], T[:, r, 0:H * W])
                                nc.vector.tensor_tensor(z[:, bass.ds(t * H, H)], T[:, r, 0:H * W].rearrange("p (h w) -> p h w", h=H)[:, :, DH],
                                                        T[:, r, H * W:NW], ALU.add)
                    if l == 0:
                        nc.vector.memset(stats[:, 0, :], 0.0).then_inc(S(p + "z"), 1)
                        v.wait_ge(S(p + "z"), 1)
                        nc.vector.scalar_tensor_tensor(mrun[l][:, :], z[:, :], SLOPES[l], z[:, :], ALU.mult, ALU.max)
                        nc.vector.memset(acc[:, :].rearrange("p (t w) -> p t w", w=W)[:, :, DH:W], 1.0)

        def attention(l, acc, sc):
            H = HEADS[l]
            DH = D // H
            W = DH + 1
            HW = H * W
            slope = SLOPES[l]
            p = f"g{l}_"
            XE_LAST = 0
            pack = sb(p + "pack", [P, RING, Q, 2], I32, sc)
            drow = sb(p + "drow", [2, 2, 2, UE], BF16, sc)
            qe = sb(p + "qe", [P, RING, Q], F32, sc)
            G = sb(p + "G", [P, RING, Q, HW], F32, sc)
            MR = 4 if l == 0 else 2
            M = sb(p + "M", [P, MR, Q, TN], F32, sc)
            MB = sb(p + "MB", [P, RING, Q, TN], BF16, sc)
            MT = sb(p + "MT", [TN, 2, 2, C, P], BF16, sc)
            mt_d = sb(p + "mt_d", [TN, 2, C, P], F32, sc)
            dloc = sb(p + "dloc", [P, 2, Q, H], F32, sc)
            b = sb(p + "b", [P, 2, Q, H], F32, sc)
            LT = sb(p + "LT", [Q * H, P], F32, sc)
            NEQ = sb(p + "NEQ", [Q * H, P + 1], F32, sc)
            FB = sb(p + "FB", [Q * H, P], F32, sc)
            RUN = sb(p + "RUN", [Q * H, P], F32, sc)
            SEL = sb(p + "SEL", [Q * H, P], F32, sc)
            RS = sb(p + "RS", [P, 4, Q, H], BF16, sc)
            RS_r = sb(p + "RS_r", [P, Q, H], F32, sc)
            sm = sb(p + "sm", [TN, Q, H], F32, sc)
            adb = sb(p + "adb", [TN, NT, 3, H], BF16, sc)
            adr = sb(p + "adr", [TN, NT, H], F32, sc)
            rhs = sb(p + "rhs", [TN, 2, 2, 3, H], BF16, sc)
            old = sb(p + "old", [TN, 2, H], F32, sc)
            mnew = sb(p + "mnew", [TN, 2, H], F32, sc)
            mres = sb(p + "mres", [TN, 2, H], F32, sc)
            XS = sb(p + "XS", [P, Q, 2, H], F32, sc)
            gone = sb(p + "gone", [TN, Q, H], F32, sc)
            top = sb(p + "top", [TN, Q, H], F32, sc)
            amax = sb(p + "amax", [TN, 2, H], F32, sc)
            zn = sb(p + "zn", [TN, 2, H], F32, sc)
            mloc = sb(p + "mloc", [TN, 2, H], F32, sc)
            adn = sb(p + "adn", [TN, 2, H], F32, sc)
            delta = sb(p + "delta", [TN, 2, H], F32, sc)
            c1 = sb(p + "c1", [TN, RING, 2, H], F32, sc)
            ze = sb(p + "ze", [P, Q, H], F32, sc)
            le = sb(p + "le", [P, Q, H], F32, sc)
            te = sb(p + "te", [P, Q, H], F32, sc)
            tm = sb(p + "tm", [P, 2, Q, H], F32, sc)
            wt = sb(p + "wt", [P, 2, Q, H], F32, sc)
            QH = Q * H
            adl, mr = ad[l], mrun[l]
            rowT_ps = bank[0][0:QH, 0:2 * P]
            V_ps = bank[6][0:TN, 0:4 * QH]
            selT_ps = bank[1][:, 0:2 * QH]
            Xe_ps = bank[7][:, 0:6 * QH]

            def run(eng, slot):
                for i in range(RING):
                    slot(i, i)
                with eng.Fori(0, BODIES - 2) as it:
                    for r in range(RING):
                        slot(it * RING + (RING + r), r)
                for i in range(SU + LAG - RING, SU + LAG):
                    slot(i, i % RING)

            def has(i, lag):
                return not isinstance(i, int) or lag <= i < SU + lag

            def late(i, k):
                return not isinstance(i, int) or i >= k

            def filled(i, r, n):
                if isinstance(i, int):
                    return (i // RING + 1) * n
                return (i - r) * (n // RING) + n

            def filled2(i, r, n):
                if isinstance(i, int):
                    return (i // 2 + 1) * n
                return (i - r % 2) * (n // 2) + n

            with nc.Block() as block:
                @block.sync
                def _(sp):
                    def slot(i, r):
                        if not has(i, 0):
                            return
                        if late(i, RING):
                            after(sp, p + f"rows_in{r}", filled(i - RING, r, 16 * Q))
                            held(sp, p + "rows_seen")
                            after(sp, p + "dloc", i - (RING - 1))
                            held(sp, p + "dloc_seen")
                        if late(i, 2):
                            after(sp, p + "spread", i - 1)
                            held(sp, p + "spread_seen")
                        if l == 1 and late(i, RING):
                            after(sp, p + "b", i - (RING - 1))
                        held(sp, p + "slot_seen")
                        for u in range(2):
                            s = sp.value_load(unit_i[0:1, bass.ds(i * 4 + 2 * u, 1)], min_val=0, max_val=E)
                            sp.dma_start(pack[:, r, u * C:(u + 1) * C, :],
                                         pack_d[bass.ds(s, UE), :].rearrange("(p c) k -> p c k", p=P)).then_inc(S(p + f"pack_in{r}"), 16)
                            sp.dma_start(drow[:, r % 2, u, :], dst_d[:, bass.ds(s, UE)]).then_inc(S(p + f"drow_in{r % 2}"), 16)
                            if l == 1:
                                sp.dma_start(qe[:, r, u * C:(u + 1) * C],
                                             q_d[bass.ds(s, UE)].rearrange("(p c) -> p c", p=P)).then_inc(S(p + f"q_in{r}"), 16)
                    run(sp, slot)

                @block.gpsimd
                def _(pool):
                    def slot(i, r):
                        if not has(i, 0):
                            return
                        pool.wait_ge(S(p + f"pack_in{r}"), filled(i, r, 32))
                        if late(i, RING):
                            after(pool, p + "summed", i * 2 - 2 * (RING - 1))
                        held(pool, p + "pool_seen")
                        for q in range(Q):
                            nc.gpsimd.indirect_dma_start(G[:, r, q, :], None, rows_d[l],
                                                         bass.IndirectOffsetOnAxis(ap=pack[:, r, q, 0:1], axis=0)).then_inc(S(p + f"rows_in{r}"), 16)
                    run(pool, slot)

                @block.tensor
                def _(pe):
                    def slot(i, r):
                        r1, r2 = (r - 1) % RING, (r - 2) % RING
                        if has(i, 0):
                            pe.wait_ge(S(p + f"drow_in{r % 2}"), filled2(i, r, 32))
                            if late(i, 1):
                                after(pe, p + "mt_abs", i)
                            for u in range(2):
                                mm = nc.tensor.matmul(bank[2 + u][0:TN, :], ones_bf[:, :], drow[:, r % 2, u, :], start=True, stop=True)
                            mm.then_inc(S(p + "spread"), 1)
                        if has(i, 1):
                            pe.wait_ge(S(p + "SEL"), i)
                            held(pe, p + "sel_seen")
                            nc.tensor.transpose(selT_ps[:, 0:QH], SEL[:, :], ident[0:QH, 0:QH])
                            nc.tensor.transpose(selT_ps[:, QH:2 * QH], NEQ[:, 1:P + 1], ident[0:QH, 0:QH]).then_inc(S(p + "selT"), 1)
                            pe.wait_ge(S(p + "RS"), i)
                            if late(i, 2):
                                after(pe, p + "top", i - 1)
                            for q in range(Q):
                                mm = nc.tensor.matmul(V_ps[:, q * 4 * H:(q + 1) * 4 * H], MB[:, r1, q, :], RS[:, :, q, :], start=True, stop=True)
                            mm.then_inc(S(p + "V"), 1)

                        def sums(u):
                            if not has(i, 2):
                                return
                            pe.wait_ge(S(p + "scaled"), i * 2 - (3 - u))
                            if l == 0:
                                pe.wait_ge(S(p + "M"), i - 1)
                            if late(i, 3):
                                after(pe, p + "acc", i * 2 - (5 - u))
                            for q in range(u * C, (u + 1) * C):
                                mm = nc.tensor.matmul(bank[4 + u][0:TN, 0:HW], M[:, r2 % MR, q, :], G[:, r2, q, :],
                                                      start=(q % C == 0), stop=(q % C == C - 1))
                            mm.then_inc(S(p + "summed"), 1)

                        if has(i, 0):
                            pe.wait_ge(S(p + "b"), i + 1)
                            if late(i, 1):
                                after(pe, p + "RUN", i)
                            held(pe, p + "b_seen")
                            nc.tensor.transpose(rowT_ps[:, 0:P], b[:, r % 2, :, :].rearrange("p q h -> p (q h)"), ident[:, :])
                            nc.tensor.transpose(rowT_ps[:, P:2 * P], dloc[:, r % 2, :, :].rearrange("p q h -> p (q h)"), ident[:, :]).then_inc(S(p + "rowT"), 1)
                        sums(0)
                        if XE_LAST:
                            sums(1)
                        if has(i, 1):
                            pe.wait_ge(S(p + "rhs"), i)
                            pe.wait_ge(S(p + "MT"), i)
                            if late(i, 2):
                                after(pe, p + "XS", i - 1)
                            for q in range(Q):
                                mm = nc.tensor.matmul(Xe_ps[:, q * 6 * H:(q + 1) * 6 * H], MT[:, r1 % 2, q // C, q % C, :],
                                                      rhs[:, q // C, :, :, :], start=True, stop=True)
                            mm.then_inc(S(p + "Xe"), 1)
                        if XE_LAST == 0:
                            sums(1)
                    run(pe, slot)

                @block.scalar
                def _(act):
                    def slot(i, r):
                        r1, r2 = (r - 1) % RING, (r - 2) % RING
                        if has(i, 1):
                            act.wait_ge(S(p + "selT"), i)
                            if late(i, 2):
                                after(act, p + "V", i - 1)
                            nc.scalar.copy(RS[:, 0:4:3, :, :].rearrange("p k q h -> p k (q h)"), selT_ps.rearrange("p (k n) -> p k n", k=2)).then_inc(S(p + "RS_hi"), 1)
                        if has(i, 2):
                            act.wait_ge(S(p + "tm"), i - 1)
                            to = wt[:, r % 2, :, :] if l == 1 else G[:, r2, :, :].rearrange("p q (h w) -> p q h w", h=H)[:, :, :, DH]
                            nc.scalar.activation(to, tm[:, r % 2, :, :], ACT.Exp).then_inc(S(p + "w"), 1)
                        if has(i, 0):
                            act.wait_ge(S(p + "spread"), i + 1)
                            if late(i, 2):
                                after(act, p + "Xe", i - 1)
                            for u in range(2):
                                ins = nc.scalar.activation(mt_d[:, u, :, :], bank[2 + u][0:TN, :].rearrange("p (e c) -> p c e", c=C), ACT.Abs,
                                                           bias=unode[0:TN, bass.ds(i * 2 + u, 1)])
                            ins.then_inc(S(p + "mt_abs"), 1)
                        if has(i, 1):
                            act.wait_ge(S(p + "delta"), i)
                            if late(i, RING):
                                after(act, p + "merged", i - (RING - 1))
                            nc.scalar.activation(c1[:, r1, :, :], delta[:, :, :], ACT.Exp).then_inc(S(p + "c1"), 1)
                        if has(i, 0):
                            act.wait_ge(S(p + "mt_abs"), i + 1)
                            nc.scalar.activation(MT[:, r % 2, :, :, :], mt_d[:, :, :, :], ACT.Relu, bias=ones[0:TN, 0:1], scale=-1.0).then_inc(S(p + "MT"), 1)
                            act.wait_ge(S(p + "rowT"), i + 1)
                            if late(i, 1):
                                after(act, p + "NEQ", i)
                            nc.scalar.copy(LT[:, :], rowT_ps[:, P:2 * P]).then_inc(S(p + "LT"), 1)
                        if has(i, 0) and l == 0:
                            act.wait_ge(S(p + "MB"), i + 1)
                            if late(i, RING):
                                after(act, p + "summed", (i - 3) * 2)
                            nc.scalar.copy(M[:, r, :, :], MB[:, r, :, :]).then_inc(S(p + "M"), 1)
                    run(act, slot)

                @block.vector
                def _(v):
                    nc.vector.memset(NEQ[:, :], 1.0).then_inc(S(p + "NEQ_set"), 1)
                    v.wait_ge(S(p + "NEQ_set"), 1)
                    V = V_ps.rearrange("p (q s h) -> p q s h", s=4, h=H)
                    adv = adl[:, :].rearrange("p (t h) -> p t h", h=H)
                    nc.vector.tensor_copy(adb[:, :, 0, :], adv).then_inc(S(p + "ad1"), 1)
                    v.wait_ge(S(p + "ad1"), 1)
                    nc.vector.tensor_tensor(adr[:, :, :], adv, adb[:, :, 0, :], ALU.subtract).then_inc(S(p + "ad1"), 1)
                    v.wait_ge(S(p + "ad1"), 2)
                    nc.vector.tensor_copy(adb[:, :, 1, :], adr[:, :, :]).then_inc(S(p + "ad1"), 1)
                    v.wait_ge(S(p + "ad1"), 3)
                    nc.vector.tensor_tensor(adb[:, :, 2, :], adr[:, :, :], adb[:, :, 1, :], ALU.subtract).then_inc(S(p + "ad1"), 1)
                    v.wait_ge(S(p + "ad1"), 4)

                    tile_regs = [[v.alloc_register(f"{p}tile{k}_{u}") for u in range(2)] for k in range(RING)]

                    def load_tiles(i, r):
                        v.reg_load(tile_regs[r], unit_j[0:1, bass.ds(i * 2, 2)])

                    def tiles(r):
                        return [v.snap(reg, min_val=0, max_val=NT - 1) for reg in tile_regs[r]]

                    def slot(i, r):
                        r1, r2, r3 = (r - 1) % RING, (r - 2) % RING, (r - 3) % RING
                        cur, one, two, three = (has(i, k) for k in range(4))
                        jm = tiles(r3) if three else None
                        jn = tiles(r1) if one else None

                        def merge(u):
                            if not three:
                                return
                            if u == 0:
                                v.wait_ge(S(p + "summed"), i * 2 - 4)
                                v.wait_ge(S(p + "c1"), i - 2)
                            if u == 1 or late(i, 4):
                                after(v, p + "acc", (i - 3) * 2 + u)
                            for h in range(H):
                                at = acc[:, bass.ds(jm[u] * HW + h * W, W)]
                                ins = nc.vector.scalar_tensor_tensor(at, at, c1[:, r3, u, h:h + 1], bank[4 + u][0:TN, h * W:(h + 1) * W],
                                                                     ALU.mult, ALU.add)
                            ins.then_inc(S(p + "acc"), 1)

                        def scale(k):
                            if not two:
                                return
                            if k == 0:
                                v.wait_ge(S(p + "w"), i - 1)
                                if l == 1:
                                    nc.vector.memset(G[:, r2, :, DH:W], 1.0)
                            if l == 0:
                                g = G[:, r2, k, :].rearrange("p (h w) -> p h w", h=H)
                                ins = nc.vector.tensor_tensor(g[:, :, 0:DH], g[:, :, 0:DH], g[:, :, DH:W].broadcast_to([P, H, DH]), ALU.mult)
                            elif k % 2 == 1:
                                ins = nc.vector.tensor_tensor(M[:, r2 % MR, k - 1:k + 1, :], MB[:, r2, k - 1:k + 1, :],
                                                              wt[:, r % 2, k - 1:k + 1, :].broadcast_to([P, 2, TN]), ALU.mult)
                            if k % C == C - 1:
                                ins.then_inc(S(p + "scaled"), 1)

                        def incidence(k):
                            if not cur:
                                return
                            if k == 0:
                                v.wait_ge(S(p + "dloc"), i + 1)
                            for q in (2 * k, 2 * k + 1):
                                ins = nc.vector.tensor_scalar(MB[:, r, q, :], iota_b[:, :], dloc[:, r % 2, q, 0:1], None, ALU.is_equal)
                            if k == 3:
                                ins.then_inc(S(p + "MB"), 1)

                        last = [None]

                        def chain(ins, name):
                            last[0] = name
                            ins.then_inc(S(p + name), 1)

                        def linked():
                            v.wait_ge(S(p + last[0]), i)

                        if one:
                            v.wait_ge(S(p + "LT"), i)
                            if late(i, 2):
                                after(v, p + "selT", i - 1)
                            nc.vector.tensor_tensor(NEQ[:, 1:P], LT[:, 1:P], LT[:, 0:P - 1], ALU.not_equal).then_inc(S(p + "NEQ"), 1)
                        if cur:
                            v.wait_ge(S(p + f"pack_in{r}"), filled(i, r, 32))
                            if late(i, 2):
                                after(v, p + "rowT", i - 1)
                            for u in range(2):
                                ins = nc.vector.tensor_scalar(dloc[:, r % 2, u * C:(u + 1) * C, :],
                                                              pack[:, r, u * C:(u + 1) * C, 1:2].bitcast(F32).broadcast_to([P, C, H]),
                                                              ubase[:, bass.ds(i * 2 + u, 1)], None, ALU.subtract)
                            ins.then_inc(S(p + "dloc"), 1)
                        if one:
                            v.wait_ge(S(p + "NEQ"), i)
                            nc.vector.tensor_scalar(FB[:, :], NEQ[:, 0:P], -BIG, None, ALU.mult).then_inc(S(p + "FB"), 1)
                            if late(i, 2):
                                after(v, p + "Xe", i - 1)
                            for u in range(2):
                                copy(rhs[:, u, 0, :, :].rearrange("p s h -> p (s h)"), adb[:, bass.ds(jn[u], 1), :, :].rearrange("p o s h -> p (o s h)"))
                            v.wait_ge(S(p + "FB"), i)
                            nc.vector.tensor_tensor_scan(RUN[:, :], FB[:, :], rowT_ps[:, 0:P], 0.0, ALU.add, ALU.max).then_inc(S(p + "RUN"), 1)
                        if two:
                            v.wait_ge(S(p + "Xe"), i - 1)
                            nc.vector.tensor_reduce(XS[:, :, :, :].rearrange("p q k h -> p (q k) h"), Xe_ps.rearrange("p (n s h) -> p n h s", s=3, h=H),
                                                    AX.X, ALU.add).then_inc(S(p + "XS"), 1)
                        if one:
                            v.wait_ge(S(p + "RUN"), i)
                            nc.vector.tensor_tensor(SEL[:, :], RUN[:, :], NEQ[:, 1:P + 1], ALU.mult).then_inc(S(p + "SEL"), 1)
                            for u in range(2):
                                copy(adn[:, u, :], adl[:, bass.ds(jn[u] * H, H)])
                        if two:
                            v.wait_ge(S(p + "XS"), i - 1)
                            nc.vector.tensor_tensor(ze[:, :, :], b[:, r % 2, :, :], XS[:, :, 0, :], ALU.add).then_inc(S(p + "ze"), 1)
                        merge(0)
                        if two:
                            v.wait_ge(S(p + "ze"), i - 1)
                            nc.vector.scalar_tensor_tensor(le[:, :, :], ze[:, :, :], slope, ze[:, :, :], ALU.mult, ALU.max).then_inc(S(p + "le"), 1)
                        if one:
                            v.wait_ge(S(p + "RS_hi"), i)
                            nc.vector.tensor_tensor(RS_r[:, :, :].rearrange("p q h -> p (q h)"), selT_ps[:, 0:QH], RS[:, 0, :, :].rearrange("p q h -> p (q h)"),
                                                    ALU.subtract).then_inc(S(p + "RS_r"), 1)
                        if two:
                            v.wait_ge(S(p + "le"), i - 1)
                            nc.vector.tensor_tensor(te[:, :, :], le[:, :, :], XS[:, :, 1, :], ALU.subtract).then_inc(S(p + "te"), 1)
                        if one:
                            v.wait_ge(S(p + "RS_r"), i)
                            nc.vector.tensor_copy(RS[:, 1, :, :], RS_r[:, :, :]).then_inc(S(p + "RS_mid"), 1)
                        if two:
                            v.wait_ge(S(p + "te"), i - 1)
                            if late(i, 4):
                                after(v, p + "w", i - 3)
                            nc.vector.tensor_scalar(tm[:, r % 2, :, :], te[:, :, :], 0.0, None, ALU.min).then_inc(S(p + "tm"), 1)
                        if one:
                            v.wait_ge(S(p + "RS_mid"), i)
                            nc.vector.tensor_tensor(RS[:, 2, :, :], RS_r[:, :, :], RS[:, 1, :, :], ALU.subtract).then_inc(S(p + "RS"), 1)
                        merge(1)
                        if one:
                            if late(i, 2):
                                after(v, p + "c1", i - 1)
                            m_at = [mr[:, bass.ds(jn[u] * H, H)] for u in range(2)]
                            if late(i, 2):
                                after(v, p + "kept1", i - 1)
                            copy(old[:, 0, :], m_at[0]).then_inc(S(p + "old0"), 1)
                            v.wait_ge(S(p + "V"), i)
                            nc.vector.tensor_reduce(sm[:, :, :], V[:, :, 0:3, :].rearrange("p q s h -> p q h s"), AX.X, ALU.add)
                            chain(nc.vector.tensor_scalar(gone[:, :, :], V[:, :, 3, :], -1.0, BIG, ALU.add, ALU.mult), "gone")
                        scale(0)
                        if one:
                            linked()
                            nc.vector.tensor_tensor(top[:, :, :], gone[:, :, :], sm[:, :, :], ALU.add).then_inc(S(p + "top"), 1)
                        if cur:
                            v.wait_ge(S(p + f"rows_in{r}"), filled(i, r, 16 * Q))
                            src_part = G[:, r, :, :].rearrange("p q (h w) -> p q h w", h=H)[:, :, :, DH]
                            if l == 0:
                                nc.vector.tensor_copy(b[:, r % 2, :, :], src_part).then_inc(S(p + "b"), 1)
                            else:
                                v.wait_ge(S(p + f"q_in{r}"), filled(i, r, 32))
                                nc.vector.tensor_tensor(b[:, r % 2, :, :], src_part, qe[:, r, :].unsqueeze(2), ALU.add).then_inc(S(p + "b"), 1)
                        scale(1)
                        if one:
                            v.wait_ge(S(p + "top"), i)
                            chain(nc.vector.tensor_reduce(amax[:, :, :], top[:, :, :].rearrange("p (u c) h -> p u h c", u=2), AX.X, ALU.max), "amax")
                        scale(2)
                        if one:
                            linked()
                            chain(nc.vector.tensor_tensor(zn[:, :, :], amax[:, :, :], adn[:, :, :], ALU.add), "zn")
                        scale(3)
                        if one:
                            linked()
                            chain(nc.vector.scalar_tensor_tensor(mloc[:, :, :], zn[:, :, :], slope, zn[:, :, :], ALU.mult, ALU.max), "mloc")
                        scale(4)
                        if one:
                            linked()
                            v.wait_ge(S(p + "old0"), i)
                            chain(nc.vector.tensor_tensor(mnew[:, 0, :], mloc[:, 0, :], old[:, 0, :], ALU.max), "mnew0")
                        scale(5)
                        if one:
                            linked()
                            chain(copy(m_at[0], mnew[:, 0, :]), "kept0")
                        scale(6)
                        if one:
                            linked()
                            chain(copy(old[:, 1, :], m_at[1]), "old1")
                        scale(7)
                        if one:
                            linked()
                            chain(nc.vector.tensor_tensor(mnew[:, 1, :], mloc[:, 1, :], old[:, 1, :], ALU.max), "mnew1")
                        if three:
                            v.wait_ge(S(p + "acc"), (i - 3) * 2 + 2)
                            v.sem_inc(S(p + "merged"), 1)
                        if one:
                            linked()
                            copy(m_at[1], mnew[:, 1, :]).then_inc(S(p + "kept1"), 1)
                            nc.vector.tensor_copy(rhs[:, :, 1, 0, :], mnew[:, :, :]).then_inc(S(p + "m_hi"), 1)
                            nc.vector.tensor_tensor(delta[:, :, :], old[:, :, :], mnew[:, :, :], ALU.subtract).then_inc(S(p + "delta"), 1)
                        incidence(0)
                        if one:
                            v.wait_ge(S(p + "m_hi"), i)
                            nc.vector.tensor_tensor(mres[:, :, :], mnew[:, :, :], rhs[:, :, 1, 0, :], ALU.subtract).then_inc(S(p + "mres"), 1)
                        incidence(1)
                        if one:
                            v.wait_ge(S(p + "mres"), i)
                            nc.vector.tensor_copy(rhs[:, :, 1, 1, :], mres[:, :, :]).then_inc(S(p + "m_mid"), 1)
                        incidence(2)
                        if has(i, 0):
                            load_tiles(i, r)
                        if one:
                            v.wait_ge(S(p + "m_mid"), i)
                            nc.vector.tensor_tensor(rhs[:, :, 1, 2, :], mres[:, :, :], rhs[:, :, 1, 1, :], ALU.subtract).then_inc(S(p + "rhs"), 1)
                        incidence(3)

                    run(v, slot)

        def finish_attention(l, acc, sc):
            H = HEADS[l]
            DH = D // H
            W = DH + 1
            HW = H * W
            p = f"f{l}_"
            bias = sb(p + "bias", [TN, D], F32, sc)
            den = sb(p + "den", [TN, NT * H], F32, sc)
            y = sb(p + "y", [TN, 2, D], F32, sc)
            with nc.Block() as block:
                @block.sync
                def _(sp):
                    sp.dma_start(bias[:, :], a[f"L{l}_gnn_bias"].rearrange("(o d) -> o d", o=1).broadcast_to([TN, D])).then_inc(S(p + "bias"), 16)

                @block.vector
                def _(v):
                    nc.vector.tensor_scalar(den[:, :], acc[:, :].rearrange("p (t w) -> p t w", w=W)[:, :, DH], 1e-30, None, ALU.max).then_inc(S(p + "den"), 1)
                    v.wait_ge(S(p + "den"), 1)
                    nc.vector.reciprocal(den[:, :], den[:, :]).then_inc(S(p + "den"), 1)
                    v.wait_ge(S(p + "den"), 2)
                    v.wait_ge(S(p + "bias"), 16)
                    with v.Fori(0, NT // 2) as h:
                        for r in range(2):
                            t = h * 2 + r
                            nc.vector.tensor_tensor(y[:, r, :].rearrange("p (h w) -> p h w", h=H),
                                                    acc[:, bass.ds(t * HW, HW)].rearrange("p (h w) -> p h w", h=H)[:, :, 0:DH],
                                                    den[:, bass.ds(t * H, H)].unsqueeze(2).broadcast_to([TN, H, DH]), ALU.mult)
                            nc.vector.tensor_tensor(X[:, bass.ds(t, 1), :].rearrange("p o d -> p (o d)"), X[:, bass.ds(t, 1), :].rearrange("p o d -> p (o d)"),
                                                    bias[:, :], ALU.add).then_inc(S(p + "y"), 1)
                        for r in range(2):
                            t = h * 2 + r
                            xt = X[:, bass.ds(t, 1), :].rearrange("p o d -> p (o d)")
                            v.wait_ge(S(p + "y"), h * 2 + 2)
                            nc.vector.tensor_tensor(xt, xt, y[:, r, :], ALU.add).then_inc(S(p + "x"), 1)
                        for r in range(2):
                            t = h * 2 + r
                            v.wait_ge(S(p + "x"), h * 2 + (r + 1))
                            held(v, p + "x_seen")
                            nc.vector.bn_stats(stats[:, r, :], X[:, bass.ds(t, 1), :].rearrange("p o d -> p (o d)")).then_inc(S(p + "s"), 1)
                        for r in range(2):
                            v.wait_ge(S(p + "s"), h * 2 + (r + 1))
                            held(v, p + "s_seen")
                            nc.vector.bn_aggr(aggr[:, r, :], stats[:, r, :]).then_inc(S(p + "aggr"), 1)
                        for r in range(2):
                            v.wait_ge(S(p + "aggr"), h * 2 + (r + 1))
                            copy(mv[:, bass.ds(h * 2 + r, 1), :].rearrange("p o d -> p (o d)"), aggr[:, r, :])

        def experts(l, sc):
            NX = EXPERTS[l]
            p = f"e{l}_"
            wr = sb(p + "wr", [P, 2, P if l == 0 else NX], F32, sc)
            wr2 = sb(p + "wr2", [P, NX], F32, sc)
            br1 = sb(p + "br1", [P, 1], F32, sc)
            br = sb(p + "br", [TN, NX], F32, sc)
            w1 = sb(p + "w1", [P, 2, NX, D], F32, sc)
            w2 = sb(p + "w2", [P, 2, NX, D], F32, sc)
            w3 = sb(p + "w3", [P, 2, NX, D], F32, sc)
            bo = sb(p + "bo", [NX, D], F32, sc)
            NQ = (2, 10)[l]
            names = (("L0_ffn_expert_b1", "L0_ffn_expert_b2"),
                     tuple("L1_ffn_" + n for n in ("b1", "g1", "be1", "m1", "v1", "b2", "g2", "be2", "m2", "v2")))[l]
            tab_r = sb(p + "tab_r", [NQ * NX, D], F32, sc)
            tab = sb(p + "tab", [P, 2, NQ, NX], F32, sc)
            sc_c = sb(p + "sc_c", [P, 2, 2, NX], F32, sc)
            bi_c = sb(p + "bi_c", [P, 2, 2, NX], F32, sc)
            before = sb(p + "before", [TN, NX, NX], F32, sc)
            xn = sb(p + "xn", [TN, GT, D], F32, sc)
            xnT = sb(p + "xnT", [P, 2, 2, GN], F32, sc)
            rhT = sb(p + "rhT", [P, GN], F32, sc)
            lg = sb(p + "lg", [TN, GT, NX], F32, sc)
            lmax = sb(p + "lmax", [TN, GT, 1], F32, sc)
            ex = sb(p + "ex", [TN, GT, NX], F32, sc)
            es = sb(p + "es", [TN, GT, 1], F32, sc)
            gt = sb(p + "gt", [TN, GT, NX, NX], F32, sc)
            eq = sb(p + "eq", [TN, GT, NX, NX], F32, sc)
            rank = sb(p + "rank", [TN, GT, NX], F32, sc)
            cw = sb(p + "cw", [TN, 2, GT, NX], F32, sc)
            cwT = sb(p + "cwT", [NX, GT, TN], F32, sc)
            h1 = sb(p + "h1", [P, 2, GN], F32, sc)
            h2 = sb(p + "h2", [P, 2, 2, GN], F32, sc)
            NXT = NG + 1
            wn = (("L0_ffn_expert_w1", "L0_ffn_expert_w2", "L0_ffn_expert_w3"), ("L1_ffn_W1", "L1_ffn_W2", "L1_ffn_Wo"))[l]
            out_v = out.rearrange("(t p) d -> p t d", p=TN)
            NGATE = 12

            def run(eng, slot):
                slot(0, 0)
                slot(1, 1)
                with eng.Fori(0, (NXT - 4) // 2) as it:
                    for r in range(2):
                        slot(it * 2 + (2 + r), r)
                slot(NXT - 2, 0)
                slot(NXT - 1, 1)

            def isprep(i):
                return not isinstance(i, int) or i < NG

            def isexp(i):
                return not isinstance(i, int) or i >= 1

            def col(name):
                return a[name].rearrange("e (k p) -> p e k", p=P)

            with nc.Block() as block:
                @block.sync
                def _(sp):
                    n = 0
                    for w, name in zip((w1, w2, w3), wn):
                        for k in range(2):
                            sp.dma_start(w[:, k, :, :], a[name][:, k * P:(k + 1) * P, :].rearrange("e p n -> p e n")).then_inc(S(p + "w"), 16)
                    if l == 0:
                        sp.dma_start(bo[:, :], a["L0_ffn_expert_b3"]).then_inc(S(p + "w"), 16)
                    else:
                        sp.dma_start(bo[:, :], a["L1_ffn_bo"]).then_inc(S(p + "w"), 16)
                        def flush(i, r):
                            if isexp(i):
                                sp.wait_ge(S(p + "group"), i)
                                held(sp, p + "group_seen")
                                sp.dma_start(out_v[:, bass.ds((i - 1) * GT, GT), :], X[:, bass.ds((i - 1) * GT, GT), :]).then_inc(S("out_done"), 16)
                        run(sp, flush)
                        sp.wait_ge(S("out_done"), 16 * NG)

                @block.gpsimd
                def _(pool):
                    nc.gpsimd.memset(before[:, :, :], 1.0).then_inc(S(p + "before"), 1)
                    pool.wait_ge(S(p + "before"), 1)
                    nc.gpsimd.affine_select(out=before[:, :, :], in_=before[:, :, :], compare_op=ALU.is_gt, fill=0.0, base=0,
                                            pattern=[[1, NX], [-1, NX]], channel_multiplier=0).then_inc(S(p + "before"), 1)

                @block.tensor
                def _(pe):
                    pe.wait_ge(S(p + "w"), 16 * 7)
                    pe.wait_ge(S(p + "sw"), 16 * (NQ + (4, 2)[l]))
                    for k in range(2):
                        mm = nc.tensor.transpose(bank[0][:, k * P:k * P + NQ * NX], tab_r[:, k * P:(k + 1) * P], ident[0:NQ * NX, 0:NQ * NX])
                    mm.then_inc(S(p + "tab_mm"), 1)
                    pe.wait_ge(S(p + "small"), 1)

                    def slot(i, r):
                        g = 1 - r

                        def prep(k):
                            if not isprep(i):
                                return
                            if k == 0:
                                pe.wait_ge(S(p + "xn"), i + 1)
                                if not isinstance(i, int) or i >= 1:
                                    after(pe, p + "b3", i)
                                for u in range(GT):
                                    for kk in range(2):
                                        mm = nc.tensor.transpose(bank[6][:, kk * 256 + u * TN:kk * 256 + (u + 1) * TN], xn[:, u, kk * P:(kk + 1) * P],
                                                                 ident[0:TN, 0:TN])
                                mm.then_inc(S(p + "xT"), 1)
                            if k == 1:
                                pe.wait_ge(S(p + "xnT"), i + 1)
                                if l == 0:
                                    for kk in range(2):
                                        mm = nc.tensor.matmul(bank[7][:, 0:GN], wr[:, kk, :], xnT[:, r, kk, :], start=(kk == 0), stop=(kk == 1))
                                    mm.then_inc(S(p + "rh_mm"), 1)
                            if k == 2:
                                if l == 0:
                                    pe.wait_ge(S(p + "rhT"), i + 1)
                                    for u in range(GT):
                                        mm = nc.tensor.matmul(bank[7][0:TN, 256 + u * 16:256 + u * 16 + NX], rhT[:, u * TN:(u + 1) * TN], wr2[:, :],
                                                              start=True, stop=True)
                                else:
                                    for u in range(GT):
                                        for kk in range(2):
                                            mm = nc.tensor.matmul(bank[7][0:TN, 256 + u * 16:256 + u * 16 + NX], xnT[:, r, kk, u * TN:(u + 1) * TN],
                                                                  wr[:, kk, :], start=(kk == 0), stop=(kk == 1))
                                mm.then_inc(S(p + "lg_mm"), 1)
                            if k == 4:
                                pe.wait_ge(S(p + "cw"), i + 1)
                                for u in range(GT):
                                    mm = nc.tensor.transpose(bank[7][0:NX, u * P:u * P + TN], cw[:, r, u, :], ident[0:TN, 0:TN])
                                mm.then_inc(S(p + "cwT_mm"), 1)
                            if k == 5:
                                pe.wait_ge(S(p + "cwT"), i + 1)
                                for u in range(GT):
                                    mm = nc.tensor.matmul(bank[6][0:TN, u * 256:u * 256 + D], cwT[:, u, :], bo[:, :], start=True, stop=True)
                                mm.then_inc(S(p + "b3_mm"), 1)

                        def layer1(e):
                            if not isexp(i):
                                return
                            if e or not isinstance(i, int) or i >= 2:
                                after(pe, p + "h1", (i - 1) * NX + e)
                            for m in range(2):
                                for kk in range(2):
                                    mm = nc.tensor.matmul(bank[m][:, 0:GN], w1[:, kk, e, m * P:(m + 1) * P], xnT[:, g, kk, :], start=(kk == 0), stop=(kk == 1))
                            mm.then_inc(S(p + "h1_mm"), 1)

                        def layer2(e):
                            if not isexp(i):
                                return
                            pe.wait_ge(S(p + "h1"), (i - 1) * NX + (e + 1))
                            if e or not isinstance(i, int) or i >= 2:
                                after(pe, p + "h2", (i - 1) * NX + e)
                            for m in range(2):
                                for kk in range(2):
                                    mm = nc.tensor.matmul(bank[2 + m][:, 0:GN], w2[:, kk, e, m * P:(m + 1) * P], h1[:, kk, :], start=(kk == 0), stop=(kk == 1))
                            mm.then_inc(S(p + "h2_mm"), 1)

                        def layer3(e):
                            if not isexp(i):
                                return
                            pe.wait_ge(S(p + "h2"), (i - 1) * NX + (e + 1))
                            if e or not isinstance(i, int) or i >= 2:
                                after(pe, p + "o", (i - 1) * NX + e)
                            for u in range(GT):
                                for kk in range(2):
                                    mm = nc.tensor.matmul(bank[4 + u][0:TN, 0:D], h2[:, e % 2, kk, u * TN:(u + 1) * TN], w3[:, kk, e, :],
                                                          start=(kk == 0), stop=(kk == 1))
                            mm.then_inc(S(p + "o_mm"), 1)

                        prep(0)
                        for e in range(NX + 1):
                            if e == 0:
                                layer1(0)
                            else:
                                layer2(e - 1)
                                if e < NX:
                                    layer1(e)
                                layer3(e - 1)
                            prep(e + 1)
                    run(pe, slot)

                @block.scalar
                def _(act):
                    if l == 0:
                        act.dma_start(wr[:, :, :], a["L0_ffn_router_w1"].rearrange("(k p) n -> p k n", p=P)).then_inc(S(p + "sw"), 16)
                        act.dma_start(wr2[:, :], a["L0_ffn_router_w2"]).then_inc(S(p + "sw"), 16)
                        act.dma_start(br1[:, :], a["L0_ffn_router_b1"].rearrange("(p o) -> p o", o=1), allow_slow_non_contiguous=True).then_inc(S(p + "sw"), 16)
                        act.dma_start(br[:, :], a["L0_ffn_router_b2"].rearrange("(o n) -> o n", o=1).broadcast_to([TN, NX])).then_inc(S(p + "sw"), 16)
                        nsw = 16 * (4 + NQ)
                    else:
                        act.dma_start(wr[:, :, :], a["L1_ffn_Wr"].rearrange("(k p) n -> p k n", p=P)).then_inc(S(p + "sw"), 16)
                        act.dma_start(br[:, :], a["L1_ffn_br"].rearrange("(o n) -> o n", o=1).broadcast_to([TN, NX])).then_inc(S(p + "sw"), 16)
                        nsw = 16 * (2 + NQ)
                    for q, nm in enumerate(names):
                        act.dma_start(tab_r[q * NX:(q + 1) * NX, :], a[nm]).then_inc(S(p + "sw"), 16)
                    act.wait_ge(S(p + "sw"), nsw)
                    act.wait_ge(S(p + "tab_mm"), 1)
                    nc.scalar.copy(tab[:, :, :, :].rearrange("p k q e -> p k (q e)"),
                                   bank[0][:, 0:2 * P].rearrange("p (k n) -> p k n", k=2)[:, :, 0:NQ * NX]).then_inc(S(p + "tab"), 1)
                    act.wait_ge(S(p + "tab"), 1)
                    if l == 1:
                        for q in range(2):
                            ins = nc.scalar.activation(sc_c[:, q, :, :], tab[:, :, 5 * q + 4, :], ACT.Sqrt, bias=eps_bn[:, :])
                        ins.then_inc(S(p + "bn_std"), 1)
                    act.wait_ge(S(p + "small"), 1)

                    def slot(i, r):
                        def prep(k):
                            if not isprep(i):
                                return
                            if k == 0:
                                act.wait_ge(S(p + "xT"), i + 1)
                                nc.scalar.copy(xnT[:, r, :, :], bank[6][:, :].rearrange("p (k n) -> p k n", k=2)[:, :, 0:GN]).then_inc(S(p + "xnT"), 1)
                            if k == 2 and l == 0:
                                act.wait_ge(S(p + "rh_mm"), i + 1)
                                nc.scalar.activation(rhT[:, :], bank[7][:, 0:GN], ACT.Relu, bias=br1[:, :]).then_inc(S(p + "rhT"), 1)
                            if k == 3:
                                act.wait_ge(S(p + "gate"), i * NGATE + 3)
                                nc.scalar.activation(ex[:, :, :], lg[:, :, :], ACT.Exp).then_inc(S(p + "ex"), 1)
                                if l == 0:
                                    act.wait_ge(S(p + "gate"), i * NGATE + NGATE)
                                    nc.scalar.activation(ex[:, :, :], lg[:, :, :], ACT.Exp).then_inc(S(p + "ex2"), 1)
                            if k == 5:
                                act.wait_ge(S(p + "cwT_mm"), i + 1)
                                nc.scalar.copy(cwT[:, :, :], bank[7][0:NX, 0:2 * P].rearrange("p (u n) -> p u n", u=GT)[:, :, 0:TN]).then_inc(S(p + "cwT"), 1)

                        def relu(e, q):
                            if not isexp(i):
                                return
                            dst = h1 if q == 0 else h2[:, e % 2, :, :]
                            act.wait_ge(S(p + f"h{q + 1}_mm"), (i - 1) * NX + (e + 1))
                            if q == 0 and (e or not isinstance(i, int) or i >= 2):
                                after(act, p + "h2_mm", (i - 1) * NX + e)
                            if q == 1 and (e >= 2 or not isinstance(i, int) or i >= 2):
                                after(act, p + "o_mm", (i - 1) * NX + (e - 1))
                            for m in range(2):
                                if l == 0:
                                    ins = nc.scalar.activation(dst[:, m, :], bank[2 * q + m][:, 0:GN], ACT.Relu, bias=tab[:, m, q, e:e + 1])
                                else:
                                    ins = nc.scalar.activation(dst[:, m, :], bank[2 * q + m][:, 0:GN], ACT.Relu, bias=bi_c[:, q, m, e:e + 1],
                                                               scale=sc_c[:, q, m, e:e + 1])
                            ins.then_inc(S(p + f"h{q + 1}"), 1)

                        prep(0)
                        for e in range(NX + 1):
                            if e == 0:
                                relu(0, 0)
                            else:
                                relu(e - 1, 1)
                                if e < NX:
                                    relu(e, 0)
                            prep(e + 1)
                    run(act, slot)

                @block.vector
                def _(v):
                    if l == 1:
                        v.wait_ge(S(p + "bn_std"), 1)
                        k = [0]

                        def step(ins):
                            k[0] += 1
                            ins.then_inc(S(p + "bn"), 1)
                            v.wait_ge(S(p + "bn"), k[0])

                        for q in range(2):
                            o = 5 * q
                            step(nc.vector.reciprocal(sc_c[:, q, :, :], sc_c[:, q, :, :]))
                            step(nc.vector.tensor_tensor(sc_c[:, q, :, :], sc_c[:, q, :, :], tab[:, :, o + 1, :], ALU.mult))
                            step(nc.vector.tensor_tensor(bi_c[:, q, :, :], tab[:, :, o, :], tab[:, :, o + 3, :], ALU.subtract))
                            step(nc.vector.tensor_tensor(bi_c[:, q, :, :], bi_c[:, q, :, :], sc_c[:, q, :, :], ALU.mult))
                            step(nc.vector.tensor_tensor(bi_c[:, q, :, :], bi_c[:, q, :, :], tab[:, :, o + 2, :], ALU.add))
                    v.wait_ge(S(p + "sw"), 16 * (NQ + (4, 2)[l]))
                    v.wait_ge(S(p + "tab"), 1)
                    v.wait_ge(S(p + "before"), 2)
                    v.sem_inc(S(p + "small"), 1)

                    def xtile(t):
                        return X[:, bass.ds(t, 1), :].rearrange("p o d -> p (o d)")

                    def slot(i, r):
                        g = 1 - r
                        n = [0]

                        def gate(ins):
                            n[0] += 1
                            ins.then_inc(S(p + "gate"), 1)
                            v.wait_ge(S(p + "gate"), i * NGATE + n[0])

                        def prep(k):
                            if not isprep(i):
                                return
                            if k == 0:
                                if not isinstance(i, int) or i >= 1:
                                    after(v, p + "xT", i)
                                for u in range(GT):
                                    t = i * GT + u
                                    ins = nc.vector.tensor_scalar(xn[:, u, :], xtile(t), mv[:, bass.ds(t, 1), 0:1].rearrange("p o d -> p (o d)"),
                                                                  rstd[:, bass.ds(t, 1)], ALU.subtract, ALU.mult)
                                ins.then_inc(S(p + "xn"), 1)
                            if k == 3:
                                v.wait_ge(S(p + "lg_mm"), i + 1)
                                L = bank[7][0:TN, 256:256 + 16 * GT].rearrange("p (u n) -> p u n", u=GT)[:, :, 0:NX]
                                gate(nc.vector.tensor_tensor(lg[:, :, :], L, br[:, :].unsqueeze(1).broadcast_to([TN, GT, NX]), ALU.add))
                                gate(nc.vector.tensor_reduce(lmax[:, :, 0], lg[:, :, :], AX.X, ALU.max))
                                gate(nc.vector.tensor_tensor(lg[:, :, :], lg[:, :, :], lmax[:, :, :].broadcast_to([TN, GT, NX]), ALU.subtract))
                                v.wait_ge(S(p + "ex"), i + 1)
                                gate(nc.vector.tensor_reduce(es[:, :, 0], ex[:, :, :], AX.X, ALU.add))
                                gate(nc.vector.reciprocal(es[:, :, :], es[:, :, :]))
                                if l == 1:
                                    after(v, p + "o", (i - 1) * NX) if not isinstance(i, int) or i >= 2 else None
                                    nc.vector.tensor_tensor(cw[:, r, :, :], ex[:, :, :], es[:, :, :].broadcast_to([TN, GT, NX]), ALU.mult).then_inc(S(p + "cw"), 1)
                                    for _ in range(NGATE - 5):
                                        n[0] += 1
                                    v.sem_inc(S(p + "gate"), NGATE - 5)
                                else:
                                    gate(nc.vector.tensor_tensor(ex[:, :, :], ex[:, :, :], es[:, :, :].broadcast_to([TN, GT, NX]), ALU.mult))
                                    for u in range(GT):
                                        pe_, pf_ = ex[:, u, :].unsqueeze(2).broadcast_to([TN, NX, NX]), ex[:, u, :].unsqueeze(1).broadcast_to([TN, NX, NX])
                                        nc.vector.tensor_tensor(gt[:, u, :, :], pf_, pe_, ALU.is_gt)
                                        ins = nc.vector.tensor_tensor(eq[:, u, :, :], pf_, pe_, ALU.is_equal)
                                    gate(ins)
                                    gate(nc.vector.tensor_tensor(eq[:, :, :, :], eq[:, :, :, :], before[:, :, :].unsqueeze(1).broadcast_to([TN, GT, NX, NX]), ALU.mult))
                                    gate(nc.vector.tensor_tensor(gt[:, :, :, :], gt[:, :, :, :], eq[:, :, :, :], ALU.add))
                                    gate(nc.vector.tensor_reduce(rank[:, :, :], gt[:, :, :, :], AX.X, ALU.add))
                                    gate(nc.vector.tensor_reduce(lmax[:, :, 0], ex[:, :, :], AX.X, ALU.max))
                                    gate(nc.vector.tensor_tensor(lg[:, :, :], ex[:, :, :], lmax[:, :, :].broadcast_to([TN, GT, NX]), ALU.subtract))
                            if k == 4 and l == 0:
                                v.wait_ge(S(p + "ex2"), i + 1)
                                nc.vector.scalar_tensor_tensor(lg[:, :, :], rank[:, :, :], 1.5, ex[:, :, :], ALU.is_lt, ALU.mult).then_inc(S(p + "g2"), 1)
                                v.wait_ge(S(p + "g2"), i * 3 + 1)
                                nc.vector.tensor_reduce(es[:, :, 0], lg[:, :, :], AX.X, ALU.add).then_inc(S(p + "g2"), 1)
                                v.wait_ge(S(p + "g2"), i * 3 + 2)
                                nc.vector.reciprocal(es[:, :, :], es[:, :, :]).then_inc(S(p + "g2"), 1)
                                v.wait_ge(S(p + "g2"), i * 3 + 3)
                                nc.vector.tensor_tensor(cw[:, r, :, :], lg[:, :, :], es[:, :, :].broadcast_to([TN, GT, NX]), ALU.mult).then_inc(S(p + "cw"), 1)
                            if k == 6:
                                v.wait_ge(S(p + "b3_mm"), i + 1)
                                for u in range(GT):
                                    xt = xtile(i * GT + u)
                                    ins = nc.vector.tensor_tensor(xt, xt, bank[6][0:TN, u * 256:u * 256 + D], ALU.add)
                                ins.then_inc(S(p + "b3"), 1)

                        def collect(e):
                            if not isexp(i):
                                return
                            v.wait_ge(S(p + "o_mm"), (i - 1) * NX + (e + 1))
                            if e == 0:
                                v.wait_ge(S(p + "b3"), i)
                            else:
                                v.wait_ge(S(p + "o"), (i - 1) * NX + e)
                            for u in range(GT):
                                xt = xtile((i - 1) * GT + u)
                                ins = nc.vector.scalar_tensor_tensor(xt, bank[4 + u][0:TN, 0:D], cw[:, g, u, e:e + 1], xt, ALU.mult, ALU.add)
                            ins.then_inc(S(p + "o"), 1)

                        prep(0)
                        for e in range(NX + 1):
                            if e >= 1:
                                collect(e - 1)
                            prep(e + 1)
                        if isexp(i):
                            v.wait_ge(S(p + "o"), (i - 1) * NX + NX)
                            v.sem_inc(S(p + "group"), 1)
                    run(v, slot)

        for l in (0, 1):
            x_stats()
            with ExitStack() as s1:
                acc = sb(f"acc{l}", [TN, NT * HEADS[l] * (D // HEADS[l] + 1)], F32, s1)
                for part in (node_rows, attention, finish_attention):
                    with ExitStack() as s2:
                        part(l, acc, s2)
                    end_stage()
            sqrt_stats()
            with ExitStack() as s1:
                experts(l, s1)
            end_stage()


def kernel(**inputs):
    import concourse.bacc as bacc
    from concourse.bass_utils import run_bass_kernel_spmd

    nc = bacc.Bacc("TRN2", target_bir_lowering=False, num_devices=1)
    arrays, aps = {}, {}
    for name in inputs:
        v = np.ascontiguousarray(inputs[name])
        arrays[f"in_{name}"] = v
        aps[name] = nc.dram_tensor(f"in_{name}", v.shape, mybir.dt.from_np(v.dtype), kind="ExternalInput").ap()
    out = nc.dram_tensor("out_x", (N, D), F32, kind="ExternalOutput").ap()
    build(nc, aps, out)
    r = run_bass_kernel_spmd(nc, [arrays], core_ids=[0])
    return r.results[0]["out_x"]
```
